# Optimizing a Trainium2 kernel written in Bass

```python
import numpy as np
import jax
import jax.numpy as jnp

def _softmax(x, axis=-1):
    return jax.nn.softmax(x, axis=axis)

def _gelu(x):
    return jax.nn.gelu(x, approximate=True)

def _silu(x):
    return jax.nn.silu(x)

def _sigmoid(x):
    return jax.nn.sigmoid(x)

def _layernorm(x, axis=-1, eps=1e-05):
    m = jnp.mean(x, axis=axis, keepdims=True)
    v = jnp.var(x, axis=axis, keepdims=True)
    return (x - m) / jnp.sqrt(v + eps)

def _scatter_add(tgt, idx, src, axis=0):
    return tgt.at[idx].add(src)

def _segment_sum(src, seg, n):
    return jax.ops.segment_sum(src, seg, n)
kernel_name = 'mk_seq_preln_d2_jaxref_r8_a28fab'

def setup_inputs(seed: int=0):
    np.random.seed(seed)
    _w = jnp.asarray

    def _L0_attn_setup():
        import jax, jax.numpy as jnp
        import numpy as np
        import math
        D_MODEL = 256
        N_HEADS = 16
        D_HEAD = D_MODEL // N_HEADS
        MAX_T = 256
        B, T = (2, 256)

        def rotate_half(x):
            x1 = x[..., ::2]
            x2 = x[..., 1::2]
            return jnp.stack((-x2, x1), axis=-1).reshape(x.shape)
        key = jax.random.key(seed)
        k1, k2, k3 = jax.random.split(key, 3)
        x = jax.random.normal(k1, (B, T, D_MODEL), dtype=jnp.float32)
        s = 1.0 / math.sqrt(D_MODEL)
        Wqkv = jax.random.uniform(k2, (3 * D_MODEL, D_MODEL), dtype=jnp.float32, minval=-s, maxval=s)
        WO = jax.random.uniform(k3, (D_MODEL, D_MODEL), dtype=jnp.float32, minval=-s, maxval=s)
        return {'x': x, 'Wqkv': Wqkv, 'WO': WO}
    _L0_attn_in = _L0_attn_setup()

    def _L0_ffn_setup():
        import jax, jax.numpy as jnp
        import numpy as np
        TOP_K = 2
        key = jax.random.key(seed)
        ks = jax.random.split(key, 5)
        B, S, D, M, E = (4, 256, 256, 256, 8)
        x = jax.random.normal(ks[0], (B, S, D), dtype=jnp.float32)
        gate_kernel = jax.random.normal(ks[1], (D, E), dtype=jnp.float32) / np.sqrt(D)
        wi_0 = jax.random.normal(ks[2], (E, D, M), dtype=jnp.float32) / np.sqrt(D)
        wi_1 = jax.random.normal(ks[3], (E, D, M), dtype=jnp.float32) / np.sqrt(D)
        wo = jax.random.normal(ks[4], (E, M, D), dtype=jnp.float32) / np.sqrt(M)
        return {'x': x, 'gate_kernel': gate_kernel, 'wi_0': wi_0, 'wi_1': wi_1, 'wo': wo}
    _L0_ffn_in = _L0_ffn_setup()

    def _L1_attn_setup():
        import jax, jax.numpy as jnp
        import numpy as np
        D = 256
        H = 16
        HD = D // H
        key = jax.random.key(seed)
        k1, k2, k3 = jax.random.split(key, 3)
        x = jax.random.normal(k1, (2, 256, D), dtype=jnp.float32)
        Wqkv = jax.random.normal(k2, (D, 3 * D), dtype=jnp.float32) * D ** (-0.5)
        Wo = jax.random.normal(k3, (D, D), dtype=jnp.float32) * D ** (-0.5)
        return {'x': x, 'Wqkv': Wqkv, 'Wo': Wo}
    _L1_attn_in = _L1_attn_setup()

    def _L1_ffn_setup():
        import jax, jax.numpy as jnp
        import numpy as np
        K_SKIP = 4
        NORM_TOPK = True
        key = jax.random.key(seed)
        k1, k2, k3, k4 = jax.random.split(key, 4)
        B, S, H, I, E = (1, 128, 256, 96, 64)
        hidden_states = jax.random.normal(k1, (B, S, H), dtype=jnp.float32)
        gate_weight = jax.random.normal(k2, (E, H), dtype=jnp.float32) * 0.02
        gate_up_proj = jax.random.normal(k3, (E, 2 * I, H), dtype=jnp.float32) * 0.02
        down_proj = jax.random.normal(k4, (E, H, I), dtype=jnp.float32) * 0.02
        return {'hidden_states': hidden_states, 'gate_weight': gate_weight, 'gate_up_proj': gate_up_proj, 'down_proj': down_proj}
    _L1_ffn_in = _L1_ffn_setup()
    _d = {'L0_attn_x': _L0_attn_in['x'], 'L0_attn_Wqkv': _L0_attn_in['Wqkv'], 'L0_attn_WO': _L0_attn_in['WO'], 'L0_ffn_gate_kernel': _L0_ffn_in['gate_kernel'], 'L0_ffn_wi_0': _L0_ffn_in['wi_0'], 'L0_ffn_wi_1': _L0_ffn_in['wi_1'], 'L0_ffn_wo': _L0_ffn_in['wo'], 'L1_attn_Wqkv': _L1_attn_in['Wqkv'], 'L1_attn_Wo': _L1_attn_in['Wo'], 'L1_ffn_gate_weight': _L1_ffn_in['gate_weight'], 'L1_ffn_gate_up_proj': _L1_ffn_in['gate_up_proj'], 'L1_ffn_down_proj': _L1_ffn_in['down_proj']}
    _x0 = _d['L0_attn_x']
    _d['L0_attn_x'] = jax.random.normal(jax.random.fold_in(jax.random.key(seed), 1), (8, 512, 256), dtype=_x0.dtype)
    del _x0
    return _d

def reference(L0_attn_x, L0_attn_Wqkv, L0_attn_WO, L0_ffn_gate_kernel, L0_ffn_wi_0, L0_ffn_wi_1, L0_ffn_wo, L1_attn_Wqkv, L1_attn_Wo, L1_ffn_gate_weight, L1_ffn_gate_up_proj, L1_ffn_down_proj):

    def _L0_attn_ref(x, Wqkv, WO):
        import jax, jax.numpy as jnp
        import numpy as np
        import math
        D_MODEL = 256
        N_HEADS = 16
        D_HEAD = D_MODEL // N_HEADS
        MAX_T = 256
        B, T = (2, 256)

        def rotate_half(x):
            x1 = x[..., ::2]
            x2 = x[..., 1::2]
            return jnp.stack((-x2, x1), axis=-1).reshape(x.shape)
        Bx, Tx, _ = x.shape
        pos = jnp.arange(Tx, dtype=jnp.float32)
        freqs = jnp.exp(-math.log(10000.0) * jnp.arange(0, D_HEAD, 2, dtype=jnp.float32) / D_HEAD)
        angles = pos[:, None] * freqs[None, :]
        sin = jnp.repeat(jnp.sin(angles), 2, axis=-1)
        cos = jnp.repeat(jnp.cos(angles), 2, axis=-1)
        sin = sin[None, None, :, :]
        cos = cos[None, None, :, :]
        qkv = x @ Wqkv.T
        q, k, v = jnp.split(qkv, 3, axis=-1)

        def to_heads(t):
            return t.reshape(Bx, Tx, N_HEADS, D_HEAD).transpose(0, 2, 1, 3)
        q, k, v = (to_heads(q), to_heads(k), to_heads(v))
        q = q * cos + rotate_half(q) * sin
        k = k * cos + rotate_half(k) * sin
        scores = jnp.einsum('bhqd,bhkd->bhqk', q, k) / math.sqrt(D_HEAD)
        mask = jnp.triu(jnp.full((Tx, Tx), -jnp.inf, dtype=scores.dtype), k=1)
        scores = scores + mask
        attn = jax.nn.softmax(scores, axis=-1)
        out = jnp.einsum('bhqk,bhkd->bhqd', attn, v)
        out = out.transpose(0, 2, 1, 3).reshape(Bx, Tx, D_MODEL)
        return out @ WO.T

    def _L0_ffn_ref(x, gate_kernel, wi_0, wi_1, wo):
        import jax, jax.numpy as jnp
        import numpy as np
        TOP_K = 2
        E = gate_kernel.shape[-1]
        gate_logits = jnp.einsum('bsd,de->bse', x, gate_kernel)
        top_k_weights, top_k_indices = jax.lax.top_k(gate_logits, TOP_K)
        top_k_weights = jax.nn.softmax(top_k_weights.astype(jnp.float32), axis=-1).astype(x.dtype)
        combine_w = jnp.sum(jax.nn.one_hot(top_k_indices, E, dtype=x.dtype) * top_k_weights[..., None], axis=-2)
        h0 = jnp.einsum('bsd,edm->bsem', x, wi_0)
        h1 = jnp.einsum('bsd,edm->bsem', x, wi_1)
        h = jax.nn.silu(h0) * h1 * combine_w[..., None]
        out = jnp.einsum('bsem,emd->bsd', h, wo)
        return out

    def _L1_attn_ref(x, Wqkv, Wo):
        import jax, jax.numpy as jnp
        import numpy as np
        D = 256
        H = 16
        HD = D // H
        B, S, _ = x.shape
        qkv = (x @ Wqkv).reshape(B, S, 3, H, HD)
        q = qkv[:, :, 0].transpose(0, 2, 1, 3)
        k = qkv[:, :, 1].transpose(0, 2, 1, 3)
        v = qkv[:, :, 2].transpose(0, 2, 1, 3)
        scores = jnp.einsum('bhqd,bhkd->bhqk', q, k) * HD ** (-0.5)
        causal = jnp.tril(jnp.ones((S, S), dtype=bool))
        scores = jnp.where(causal, scores, jnp.float32(-1000000000.0))
        a = jax.nn.softmax(scores, axis=-1)
        o = jnp.einsum('bhqk,bhkd->bhqd', a, v)
        o = o.transpose(0, 2, 1, 3).reshape(B, S, H * HD)
        return o @ Wo

    def _L1_ffn_ref(hidden_states, gate_weight, gate_up_proj, down_proj):
        import jax, jax.numpy as jnp
        import numpy as np
        K_SKIP = 4
        NORM_TOPK = True
        B, S, H = hidden_states.shape
        E = gate_weight.shape[0]
        x = hidden_states.reshape(-1, H)
        T = x.shape[0]
        router_logits = x @ gate_weight.T
        router_probs = jax.nn.softmax(router_logits.astype(jnp.float32), axis=-1)
        router_probs = router_probs.astype(router_logits.dtype)
        top_v, top_i = jax.lax.top_k(router_probs, K_SKIP)
        if NORM_TOPK:
            top_v = top_v / jnp.clip(top_v.sum(axis=-1, keepdims=True), 1e-12)
        combine = jnp.zeros((T, E), dtype=top_v.dtype).at[jnp.arange(T)[:, None], top_i].add(top_v)

        def body(acc, expert):
            w1, w2, we = expert
            gate, up = jnp.split(x @ w1.T, 2, axis=-1)
            h = jax.nn.silu(gate) * up @ w2.T
            return (acc + h * we[:, None], None)
        out, _ = jax.lax.scan(body, jnp.zeros_like(x), (gate_up_proj, down_proj, combine.T))
        return out.reshape(B, S, H)
    x = L0_attn_x
    x = x + _L0_attn_ref(_layernorm(x, axis=-1), L0_attn_Wqkv, L0_attn_WO)
    x = x + _L0_ffn_ref(_layernorm(x, axis=-1), L0_ffn_gate_kernel, L0_ffn_wi_0, L0_ffn_wi_1, L0_ffn_wo)
    x = x + _L1_attn_ref(_layernorm(x, axis=-1), L1_attn_Wqkv, L1_attn_Wo)
    x = x + _L1_ffn_ref(_layernorm(x, axis=-1), L1_ffn_gate_weight, L1_ffn_gate_up_proj, L1_ffn_down_proj)
    return x

_drawn_inputs = setup_inputs


def setup_inputs(seed=0):
    import zlib

    import numpy as np

    out = dict(_drawn_inputs(seed))
    spreads = {}
    factors = {'L1_ffn_gate_weight': 8.0, 'L1_ffn_gate_up_proj': 8.0, 'L1_ffn_down_proj': 8.0}
    for name, (base, spread) in spreads.items():
        noise = np.random.default_rng([zlib.crc32(name.encode()), seed]).standard_normal(out[name].shape)
        drawn = base * np.exp(spread * noise) if base else spread * noise
        out[name] = jnp.asarray(drawn.astype(out[name].dtype))
    for name, factor in factors.items():
        out[name] = (out[name] * factor).astype(out[name].dtype)
    return out
```

```python
from contextlib import ExitStack

import concourse.bass as bass
from concourse import mybir

ALU = mybir.AluOpType
ACT = mybir.ActivationFunctionType
F32 = mybir.dt.float32
BF16 = mybir.dt.bfloat16
U32 = mybir.dt.uint32
I32 = mybir.dt.int32
AX = mybir.AxisListType.X
ds = bass.ds

P = 128
B, S, D = 8, 512, 256
H, DH = 16, 16
NT = S // P
TILES = B * NT
TOK = B * S
C = D // P
HG = 4
G = H // HG
HV = 32
SCALE = float(DH) ** -0.5
EPS = 1e-5
Q_PART = (0, 0, 1, 1, 0, 2)
K_PART = (0, 1, 0, 1, 2, 0)
ROWS = DH * len(Q_PART)
EXPERTS, CHOICES, HIDDEN = (8, 64), (2, 4), (256, 96)


def blocks(layer):
    e, k = EXPERTS[layer], CHOICES[layer]
    return -(-(TOK * k // P + e - 1) // 8) * 8


BLOCKS = (blocks(0), blocks(1))
SLOTS = 8
RING = 8

PER = dict(a_stats=4, a_aggr=4, a_eps=1, a_rstd=1, a_norm=4, r_stats=4, r_aggr=4, r_eps=1, r_rstd=1,
           r_norm=4, xnT_ready=1, xnT_done=1, qkv_ready=4, qk_copied=4, v_copied=4, chunk_ready=2,
           part1=2, rest1=2, part2=2, part3=2, s1_ready=32, max_done=32, s2_ready=32, exp_done=32,
           pv_done=16, m_split=16, mT_ready=4, mT_done=4, o_copied=4, oT_ready=4, rec_done=4,
           attn_done=4, attnT_ready=1, attnT_done=1, proj_ready=1, resid_done=1, xn2T_ready=1,
           xn2T_done=1, logits_ready=1, prefix_ready=1, tok_ready=1, qk_stored=16, k_stored=16,
           xn_stored=16, rope_cos=4, rope_swap=8, rope_done=4)


def batch_units():
    u = [("xnT", "xnT_done", 1)]
    u += [(("qkv", i), "v_copied", i + 1) for i in range(NT)]
    u += [(("chunk", i), "rest1", i + 1) for i in range(2)]
    p1 = lambda g: [(("p1", g, n), "max_done", 8 * g + n + 1) for n in range(8)]
    p2 = lambda g: [(("p2", g, n), "exp_done", 8 * g + n + 1) for n in range(8)]
    u += p1(0)
    for g in range(G):
        nxt = p1(g + 1) if g + 1 < G else []
        for n, unit in enumerate(p2(g)):
            u.append(unit)
            u += nxt[n:n + 1]
        u.append((("turn", g), "attn_done", g + 1))
    u += [("attnT", "attnT_done", 1), ("proj", "resid_done", 1), ("xn2T", "xn2T_done", 1)]
    assert len(u) % 3 == 0
    return u


UNITS = batch_units()
UNIT = {name: n for n, (name, _, _) in enumerate(UNITS)}


def two_moe_layers(nc, x_in, wqkv_in, wo_in, gate_in, w01_in, wout_in, cos_in, sin_in, identf_in, identb_in,
                   masks_in, tri_in, token_in, out):
    ctx = ExitStack()
    with ctx:
        def sb(name, shape, dt=F32):
            return ctx.enter_context(nc.sbuf_tensor(name, shape, dt))

        def sem(name):
            return ctx.enter_context(nc.semaphore(name))

        def dram(name, shape, dt=F32):
            return nc.dram_tensor(name, shape, dt, kind="Internal").ap()

        parts_dram = dram("parts_dram", (2, P, 3, 2, S), BF16)
        xn_dram = dram("xn_dram", (TOK, D))
        id_dram = [dram(f"id_dram{m}", (EXPERTS[m] * TOK, 1)) for m in range(2)]
        y_dram = [dram(f"y_dram{m}", (BLOCKS[m] * P, D)) for m in range(2)]

        x = sb("x", [P, TILES, D])
        wqkv = sb("wqkv", [P, C, 3 * D])
        wo = sb("wo", [P, C, D])
        gate = [sb(f"gate{m}", [P, C, EXPERTS[m]]) for m in range(2)]
        w01 = sb("w01", [P, EXPERTS[0], C, 2 * HIDDEN[0]])
        ring1 = w01[:, :, :, :].rearrange("p e c n -> p (e c n)")[:, 0:SLOTS * 640].rearrange(
            "p (s n) -> p s n", s=SLOTS)
        q_stack = sb("q_stack", [P, H, S], BF16)
        k_stack = sb("k_stack", [P, H, S], BF16)
        values = sb("values", [P, NT, H, HV])
        probs = sb("probs", [P, 2, HG, S])
        wout = probs[:, :, :, :].rearrange("p a h s -> p (a h s)").rearrange("p (e c n) -> p e c n", e=8, c=C)
        xn = sb("xn", [P, NT, D])
        xnT = sb("xnT", [P, C, S])
        qk = sb("qk", [P, NT, 2 * D])
        oT = sb("oT", [P, S])
        attn = sb("attn", [P, NT, D])
        attnT = sb("attnT", [P, C, S])
        xn2 = sb("xn2", [P, NT, D])
        xn2T = attnT
        work = sb("work", [P, 6144])
        parts = work[:, 0:3072].bitcast(BF16).rearrange("p (a c s) -> p a c s", a=3, c=4)
        qk_raw = work[:, 3072:4096].rearrange("p (a n) -> p a n", a=2)
        rest = work[:, 4096:5120]
        rope = work[:, 5120:6144].rearrange("p (a n) -> p a n", a=2)
        xg = work[:, 0:1024].rearrange("p (r n) -> p r n", r=4)
        xgT = work[:, 1024:1536].rearrange("p (r c t) -> p r c t", r=2, c=C)
        act = work[:, 1536:2048].rearrange("p (r n) -> p r n", r=2)
        hid = work[:, 2048:2560].rearrange("p (r n) -> p r n", r=2)
        hidT = work[:, 2560:3072].rearrange("p (r c t) -> p r c t", r=2, c=C)
        y = work[:, 3072:3584].rearrange("p (r n) -> p r n", r=2)
        back = work[:, 3584:3584 + RING * D].rearrange("p (r n) -> p r n", r=RING)

        cos = sb("cos", [P, NT, DH])
        sin = sb("sin", [P, NT, DH])
        identf = sb("identf", [P, P])
        identb = sb("identb", [P, P], BF16)
        masks = sb("masks", [P, 2, P], BF16)
        tri = sb("tri", [P, 2, P], BF16)
        tri_f = sb("tri_f", [P, 3, P])
        token = sb("token", [P, TILES])
        iota_e = sb("iota_e", [P, 64])
        base_e = sb("base_e", [P, 64])
        iota_t = sb("iota_t", [P, 192])
        iota_j = sb("iota_j", [P, 32])
        iota_p = sb("iota_p", [P, 2])
        half = sb("half", [P, NT])
        zeros = probs[:, 0, :, :].rearrange("p h s -> p (h s)")
        ids_f = sb("ids_f", [P, 2, P])
        stats = {k: sb(f"{k}_st", [P, NT, 6]) for k in "ar"}
        mean_var = {k: sb(f"{k}_mv", [P, NT, 2]) for k in "ar"}
        var_eps = {k: sb(f"{k}_ve", [P, NT]) for k in "ar"}
        rstd = {k: sb(f"{k}_rs", [P, NT]) for k in "ar"}
        neg_max = sb("neg_max", [P, 2, HG, NT])
        max_rest = sb("max_rest", [P, 2, HG * NT])
        max_parts = sb("max_parts", [P, 2, 3, HG * NT], BF16)
        maxT = sb("maxT", [3 * HG * NT, 2, P], BF16)
        rec = sb("rec", [P, NT, HG])
        r_max = sb("r_max", [P, NT])
        r_exp = sb("r_exp", [P, NT, 64])
        r_sum = sb("r_sum", [P, NT])
        r_inv = sb("r_inv", [P, NT])
        r_prob = sb("r_prob", [P, NT, 64])
        top = sb("top", [P, NT, 8])
        top_i = sb("top_i", [P, NT, 8], U32)
        chosen = sb("chosen", [P, NT, 4])
        onehot = sb("onehot", [P, NT, 4, 64])
        picked = rest
        mask_e = sb("mask_e", [P, NT, 64], BF16)
        tile_sum = sb("tile_sum", [P, 64])
        before = [sb(f"before{m}", [P, EXPERTS[m]], BF16) for m in range(2)]
        place_e = sb("place_e", [P, NT, 64])
        dest_f = sb("dest_f", [P, NT, 4])
        dest = sb("dest", [P, NT, 4], U32)
        token_now = sb("token_now", [P, NT])
        dest_all = sb("dest_all", [P, TILES, 4])
        expert_all = sb("expert_all", [P, TILES, 4])
        weight_all = sb("weight_all", [P, TILES, 4])
        slot_all = sb("slot_all", [P, TILES, 4], U32)
        nblk = sb("nblk", [64, 4])
        more = sb("more", [64, 32])
        upto = sb("upto", [64, 192])
        nblk_row = sb("nblk_row", [64, P])
        onb = sb("onb", [64, 2])
        plan_f = sb("plan_f", [P, 192])
        plan_i = sb("plan_i", [P, 3, 192], I32)
        corr = sb("corr", [P, 64])
        blk_f = sb("blk_f", [P, 2, 2])
        blk_i = sb("blk_i", [P, 2], U32)
        ids = sb("ids", [P, 192], U32)
        ids_now = sb("ids_now", [P, 2, 4], U32)
        slots_now = sb("slots_now", [P, 2, RING], U32)

        ps = ctx.enter_context(nc.psum_tensor("ps", [P, 8, 512], F32))
        pair = [ps[:, 2 * i:2 * i + 2, :] for i in range(3)]
        pair_flat = [v.rearrange("p a n -> p (a n)") for v in pair]
        ps_o = ps[:, 6, :]
        ps_logits = ps[:, 7, 0:256]
        ps_prefix = ps[:, 7, 256:512]
        ps_max = ps[0:48, 7, 256:320].bitcast(BF16)

        s = {k: sem(k) for k in PER}
        const_in = sem("const_in")
        x_in0, x_in1 = sem("x_in0"), sem("x_in1")
        w_in = [sem(f"w_in{m}") for m in range(2)]
        w0_in = sem("w0_in")
        iotas = sem("iotas")
        zeroed = sem("zeroed")
        own_wait = sem("own_wait")
        stack_in = [sem(f"stack_in{g}") for g in range(G)]
        max_in = [sem(f"max_in{g}") for g in range(G)]
        ids_zero = [sem(f"ids_zero{m}") for m in range(2)]
        route = [sem(f"route{m}") for m in range(2)]
        r_exp_done = [sem(f"r_exp_done{m}") for m in range(2)]
        scattered = [sem(f"scattered{m}") for m in range(2)]
        plan_v = [sem(f"plan_v{m}") for m in range(2)]
        plan_t = [sem(f"plan_t{m}") for m in range(2)]
        blk_in = [sem(f"blk_in{m}") for m in range(2)]
        M = [{k: sem(f"{k}{m}") for k in (
            "gather0", "gather1", "gather2", "gather3", "x_turned", "xT_copied", "mm1_ready", "silu_done",
            "hid_done", "h_turned", "hT_copied", "mm2_ready", "y_copied", "y_store0", "y_store1",
            "ids_copied", "slots_copied", "back_used")} for m in range(2)]
        back_in = [sem(f"back_in{r}") for r in range(RING)]
        expert_in = sem("expert_in")
        out_sem = sem("out_sem")
        ROUTE = (24, 26)

        def at(name, nb, n):
            return nb * PER[name] + n

        block = ctx.enter_context(nc.Block())

        @block.sync
        def _(sp):
            sp.dma_start(identf[:], identf_in).then_inc(const_in, 16)
            sp.dma_start(x[:, 0:NT, :], x_in[:, 0:NT, :]).then_inc(x_in0, 16)
            sp.dma_start(wqkv[:], wqkv_in[0]).then_inc(w_in[0], 16)
            for dst, src in ((identb, identb_in), (masks, masks_in), (cos, cos_in), (sin, sin_in),
                             (tri, tri_in), (token, token_in), (gate[0], gate_in[0]), (gate[1], gate_in[1])):
                sp.dma_start(dst[:], src).then_inc(const_in, 16)
            sp.dma_start(wo[:], wo_in[0]).then_inc(w_in[0], 16)
            sp.dma_start(x[:, NT:TILES, :], x_in[:, NT:TILES, :]).then_inc(x_in1, 16)
            sp.dma_start(w01[:], w01_in[0]).then_inc(w0_in, 16)
            sp.wait_ge(zeroed, 1)
            for m in range(2):
                n = EXPERTS[m] * TOK // P
                sp.dma_start(id_dram[m].rearrange("(p a) b -> p (a b)", p=P), zeros[:, 0:n]).then_inc(ids_zero[m], 16)

            def attention(m, b):
                nb = m * B + b
                for cp, stored in ((0, "qk_stored"), (1, "k_stored")):
                    sp.wait_ge(s["part3"], at("part3", nb, cp + 1))
                    sp.dma_start(parts_dram[cp], parts[:, :, 2 * cp:2 * cp + 2, :]).then_inc(s[stored], 16)
                sp.wait_ge(s["qk_stored"], at("qk_stored", nb, 16))
                sp.wait_ge(s["k_stored"], at("k_stored", nb, 16))
                sp.sem_inc(own_wait, 1)
                sp.wait_ge(s["s2_ready"], at("s2_ready", nb, 0))
                for g in range(G):
                    for cp, stack, part in ((0, q_stack, Q_PART), (1, k_stack, K_PART)):
                        src = parts_dram[cp].rearrange("(h r) a c s -> r h a c s", r=DH)
                        for j in range(len(part)):
                            h0 = HG * g % 8
                            sp.dma_start(stack[DH * j:DH * j + DH, HG * g:HG * g + HG, :],
                                         src[:, h0:h0 + HG, part[j], HG * g // 8, :]).then_inc(stack_in[g], 16)
                for g in range(G):
                    sp.wait_ge(s["mT_done"], at("mT_done", nb, g + 1))
                    for j in range(3):
                        sp.dma_start(q_stack[ROWS + j:ROWS + j + 1, HG * g:HG * g + HG, :].rearrange(
                            "p h (a t) -> p (h a) t", t=P), maxT[16 * j:16 * j + 16, g % 2, :]).then_inc(max_in[g], 16)
                sp.wait_ge(s["r_norm"], at("r_norm", nb, NT))
                sp.sem_inc(own_wait, 1)
                sp.dma_start(xn_dram.rearrange("(i p) d -> p i d", p=P)[:, ds(NT * b, NT), :], xn2[:])\
                  .then_inc(s["xn_stored"], 16)

            for m in range(2):
                with sp.Fori(0, B) as b:
                    attention(m, b)
                if m == 0:
                    sp.wait_ge(s["pv_done"], at("pv_done", B, 0))
                    sp.dma_start(wout, wout_in[0]).then_inc(w0_in, 16)
                    sp.wait_ge(s["proj_ready"], at("proj_ready", B, 0))
                    sp.dma_start(wqkv[:], wqkv_in[1]).then_inc(w_in[1], 16)
                    sp.dma_start(wo[:], wo_in[1]).then_inc(w_in[1], 16)
                    sp.wait_ge(M[0]["mm1_ready"], BLOCKS[0])
                    sp.nop()
                else:
                    def load_expert(e, slot):
                        sp.dma_start(ring1[:, slot, 0:384], w01_in[1][e]).then_inc(expert_in, 16)
                        sp.dma_start(ring1[0:HIDDEN[1], slot, 384:640], wout_in[1][e]).then_inc(expert_in, 16)

                    for e in range(SLOTS):
                        load_expert(e, e)
                        sp.wait_ge(expert_in, 32 * (e + 1))
                    sp.wait_ge(plan_v[1], PLAN_READY)
                    with sp.Fori(1, EXPERTS[1] // SLOTS) as q:
                        for r in range(SLOTS):
                            done = sp.value_load(plan_i[0:1, 2, ds(q * SLOTS + (r - SLOTS), 1)],
                                                 min_val=0, max_val=BLOCKS[1])
                            sp.wait_ge(M[1]["mm2_ready"], done)
                            sp.sem_inc(own_wait, 1)
                            e = q * SLOTS + r
                            sp.dma_start(ring1[:, r, 0:384],
                                         w01_in[1][ds(e, 1)].rearrange("a p n -> (a p) n")).then_inc(expert_in, 16)
                            sp.dma_start(ring1[0:HIDDEN[1], r, 384:640],
                                         wout_in[1][ds(e, 1)].rearrange("a p n -> (a p) n")).then_inc(expert_in, 16)
                            sp.wait_ge(expert_in, 32 * (e + 1))
                            sp.sem_inc(own_wait, 1)
                    per = RING // CHOICES[1]
                    with sp.Fori(0, TILES // per) as q:
                        sp.wait_ge(M[1]["back_used"], (q + 1) * RING)
                        sp.sem_inc(own_wait, 1)
                        sp.dma_start(out[:, ds(q * per, per), :], x[:, ds(q * per, per), :]).then_inc(out_sem, 16)
                    sp.wait_ge(out_sem, 16 * TILES // per)

        @block.gpsimd
        def _(pool):
            pool.memset(zeros, 0.0).then_inc(zeroed, 1)
            pool.memset(half[:], -0.5).then_inc(iotas, 1)
            imprecise = dict(allow_small_or_imprecise_dtypes=True)
            pool.iota(iota_e[:], pattern=[[1, 64]], base=0, channel_multiplier=0, **imprecise).then_inc(iotas, 1)
            pool.iota(base_e[:], pattern=[[TOK, 64]], base=0, channel_multiplier=0, **imprecise).then_inc(iotas, 1)
            pool.iota(iota_t[:], pattern=[[1, 192]], base=0, channel_multiplier=0, **imprecise).then_inc(iotas, 1)
            pool.iota(iota_j[:], pattern=[[P, 32]], base=0, channel_multiplier=0, **imprecise).then_inc(iotas, 1)
            pool.iota(iota_p[:], pattern=[[P, 2]], base=0, channel_multiplier=1, **imprecise).then_inc(iotas, 1)
            pool.memset(values[:, :, :, DH:HV], 0.0).then_inc(iotas, 1)

            def rstd_of(k, nb):
                pool.wait_ge(s[f"{k}_aggr"], at(f"{k}_aggr", nb, NT))
                pool.sem_inc(own_wait, 1)
                pool.tensor_scalar(var_eps[k][:], mean_var[k][:, :, 1], EPS, None, ALU.add).then_inc(s[f"{k}_eps"], 1)
                pool.wait_ge(s[f"{k}_eps"], at(f"{k}_eps", nb, 1))
                pool.tensor_tensor(rstd[k][:], var_eps[k][:], half[:], ALU.pow).then_inc(s[f"{k}_rstd"], 1)

            def attention(m, b):
                nb = m * B + b
                rstd_of("a", nb)
                if m == 0:
                    for i in range(NT):
                        pool.wait_ge(s["qk_copied"], at("qk_copied", nb, i + 1))
                        raw = qk_raw[:, i % 2, :].rearrange("p (h j e) -> p h j e", h=2 * H, e=2)
                        swap = rope[:, 1, :].rearrange("p (h j e) -> p h j e", h=2 * H, e=2)
                        if i >= 1:
                            pool.wait_ge(s["rope_done"], at("rope_done", nb, i))
                        for e in range(2):
                            sn = sin[:, i, e::2].rearrange("p (a j) -> p a j", a=1).to_broadcast([P, 2 * H, DH // 2])
                            pool.tensor_tensor(swap[:, :, :, e], raw[:, :, :, 1 - e], sn, ALU.mult)\
                                .then_inc(s["rope_swap"], 1)
                rstd_of("r", nb)
                pool.wait_ge(scattered[m], b * (16 * NT * CHOICES[m]))
                pool.sem_inc(own_wait, 1)
                pool.tensor_copy(token_now[:], token[:, ds(NT * b, NT)]).then_inc(s["tok_ready"], 1)
                pool.wait_ge(s["tok_ready"], at("tok_ready", nb, 1))
                pool.sem_inc(own_wait, 1)
                pool.wait_ge(route[m], b * ROUTE[m] + ROUTE[m])
                pool.sem_inc(own_wait, 1)
                for i in range(NT):
                    for k in range(CHOICES[m]):
                        pool.indirect_dma_start(
                            id_dram[m], bass.IndirectOffsetOnAxis(ap=dest[:, i, k:k + 1], axis=0),
                            token_now[:, i:i + 1], None).then_inc(scattered[m], 16)

            def find_blocks(m):
                pool.wait_ge(scattered[m], B * 16 * NT * CHOICES[m])
                pool.wait_ge(plan_v[m], PLAN_BLOCKS)
                table = id_dram[m].rearrange("(r c) b -> r (c b)", c=P)
                for h in range(-(-BLOCKS[m] // P)):
                    n = min(P, BLOCKS[m] - h * P)
                    pool.indirect_dma_start(ids_f[0:n, h, :], None, table,
                                            bass.IndirectOffsetOnAxis(ap=blk_i[0:n, h:h + 1], axis=0))\
                        .then_inc(blk_in[m], 16)

            def gathers(m, q):
                for j in range(2):
                    t0 = q * 8 + 4 * j
                    first = isinstance(q, int)
                    if not first:
                        pool.wait_ge(M[m]["xT_copied"], t0 - 4)
                        pool.sem_inc(own_wait, 1)
                    pool.tensor_copy(ids_now[:, j, :], ids[:, ds(t0, 4)]).then_inc(M[m]["ids_copied"], 1)
                    pool.wait_ge(M[m]["ids_copied"], q * 2 + j + 1)
                    pool.sem_inc(own_wait, 1)
                    for r in range(4):
                        if not (first and j == 0):
                            pool.wait_ge(M[m]["xT_copied"], t0 + (r - 3))
                            pool.sem_inc(own_wait, 1)
                        pool.indirect_dma_start(xg[:, r, :], None, xn_dram,
                                                bass.IndirectOffsetOnAxis(ap=ids_now[:, j, r:r + 1], axis=0))\
                            .then_inc(M[m][f"gather{r}"], 16)

            def gathers_back(m, q):
                flat = slot_all[:, :, 0:CHOICES[m]].rearrange("p i k -> p (i k)") if CHOICES[m] == 4 else None
                for j in range(2):
                    rnd = q * 2 + j
                    if not (isinstance(q, int) and j == 0):
                        pool.wait_ge(M[m]["back_used"], rnd * RING - RING + 1)
                        pool.sem_inc(own_wait, 1)
                    per = RING // CHOICES[m]
                    pool.tensor_copy(slots_now[:, j, :].rearrange("p (i k) -> p i k", i=per),
                                     slot_all[:, ds(rnd * per, per), 0:CHOICES[m]]).then_inc(M[m]["slots_copied"], 1)
                    pool.wait_ge(M[m]["slots_copied"], rnd + 1)
                    pool.sem_inc(own_wait, 1)
                    for r in range(RING):
                        if not (isinstance(q, int) and j == 0):
                            pool.wait_ge(M[m]["back_used"], rnd * RING + (r - RING + 1))
                            pool.sem_inc(own_wait, 1)
                        pool.indirect_dma_start(back[:, r, :], None, y_dram[m],
                                                bass.IndirectOffsetOnAxis(ap=slots_now[:, j, r:r + 1], axis=0))\
                            .then_inc(back_in[r], 16)

            pool.wait_ge(const_in, 16 * 9)
            pool.wait_ge(iotas, 14)
            for m in range(2):
                pool.wait_ge(ids_zero[m], 16)
                with pool.Fori(0, B) as b:
                    attention(m, b)
                find_blocks(m)
                pool.wait_ge(plan_v[m], PLAN_IDS)
                pool.wait_ge(s["xn_stored"], 16 * B * (m + 1))
                gathers(m, 0)
                with pool.Fori(1, BLOCKS[m] // 8) as q:
                    gathers(m, q)
                for r in range(2):
                    pool.wait_ge(M[m][f"y_store{r}"], 16 * (BLOCKS[m] // 2))
                gathers_back(m, 0)
                with pool.Fori(1, TILES * CHOICES[m] // RING // 2) as q:
                    gathers_back(m, q)

        @block.tensor
        def _(pe):
            def slot(name, nb):
                n = UNIT[name]
                if n >= 3:
                    _, done, count = UNITS[n - 3]
                    pe.wait_ge(s[done], at(done, nb, count))
                else:
                    _, done, _ = UNITS[n - 3]
                    pe.wait_ge(s[done], at(done, nb, 0))
                return n % 3

            def turn_tokens(src, dst):
                for c in range(C):
                    for i in range(NT):
                        last = pe.transpose(dst[:, c, i * P:(i + 1) * P], src[:, i, c * P:(c + 1) * P], identf[:])
                return last

            def project(m, b):
                nb = m * B + b
                k = slot("xnT", nb)
                pe.wait_ge(s["a_norm"], at("a_norm", nb, NT))
                turn_tokens(xn, pair[k]).then_inc(s["xnT_ready"], 1)
                pe.wait_ge(s["xnT_done"], at("xnT_done", nb, 1))
                for i in range(NT):
                    k = slot(("qkv", i), nb)
                    for c in range(C):
                        lhs = xnT[:, c, i * P:(i + 1) * P]
                        pe.matmul(pair[k][:, 0, :], lhs, wqkv[:, c, 0:2 * D], start=(c == 0), stop=(c == C - 1))
                        last = pe.matmul(pair[k][:, 1, 0:D], lhs, wqkv[:, c, 2 * D:3 * D],
                                         start=(c == 0), stop=(c == C - 1))
                    last.then_inc(s["qkv_ready"], 1)
                for cp in range(2):
                    k = slot(("chunk", cp), nb)
                    if cp == 0:
                        done = "rope_done" if m == 0 else "qk_copied"
                        pe.wait_ge(s[done], at(done, b if m == 0 else nb, NT))
                    for half_ in range(2):
                        for i in range(NT):
                            c0 = (2 * cp + half_) * P
                            last = pe.transpose(pair[k][:, half_, i * P:(i + 1) * P], qk[:, i, c0:c0 + P], identf[:])
                    last.then_inc(s["chunk_ready"], 1)

            def first_pass(nb, g, n):
                qb, p = divmod(n, 2)
                k = slot(("p1", g, n), nb)
                if n == 0:
                    pe.wait_ge(stack_in[g], nb * (16 * 12) + 16 * 12)
                for j in range(2):
                    h = HG * g + 2 * p + j
                    pe.matmul(pair[k][:, j, 0:(qb + 1) * P], q_stack[0:ROWS, h, qb * P:(qb + 1) * P],
                              k_stack[0:ROWS, h, 0:(qb + 1) * P], start=True, stop=False)
                    last = pe.matmul(pair[k][:, j, qb * P:(qb + 1) * P], identb[:], masks[:, 0, :],
                                     start=False, stop=True)
                last.then_inc(s["s1_ready"], 1)

            def turn_max(nb, g):
                pe.wait_ge(s["m_split"], at("m_split", nb, 4 * g + 4))
                if g >= 1:
                    pe.wait_ge(s["mT_done"], at("mT_done", nb, g))
                pe.sem_inc(own_wait, 1)
                pe.transpose(ps_max, max_parts[:, g % 2, :, :].rearrange("p a n -> p (a n)"), identb[:])\
                    .then_inc(s["mT_ready"], 1)

            def second_pass(nb, g, n):
                kb, p = divmod(n, 2)
                k = slot(("p2", g, n), nb)
                if n == 0:
                    pe.wait_ge(max_in[g], nb * 48 + 48)
                cols = S - kb * P
                for j in range(2):
                    h = HG * g + 2 * p + j
                    pe.matmul(pair[k][:, j, 0:cols], k_stack[0:ROWS + 3, h, kb * P:(kb + 1) * P],
                              q_stack[0:ROWS + 3, h, kb * P:S], start=True, stop=False)
                    last = pe.matmul(pair[k][:, j, 0:P], identb[:], masks[:, 1, :], start=False, stop=True)
                last.then_inc(s["s2_ready"], 1)

            def weigh_values(nb, g, kb):
                pe.wait_ge(s["exp_done"], at("exp_done", nb, 8 * g + 2 * kb + 2))
                if kb == 0 and g >= 1:
                    pe.wait_ge(s["o_copied"], at("o_copied", nb, g))
                if kb == 0 and g == 0:
                    pe.wait_ge(s["v_copied"], at("v_copied", nb, NT))
                cols = S - kb * P
                for j in range(HG):
                    last = pe.matmul(ps_o[HV * j:HV * j + HV, kb * P:S], values[:, kb, HG * g + j, :],
                                     probs[:, kb % 2, j, 0:cols], start=(kb == 0), stop=(kb == NT - 1))
                last.then_inc(s["pv_done"], 1)

            def turn_heads(nb, g):
                k = slot(("turn", g), nb)
                pe.wait_ge(s["o_copied"], at("o_copied", nb, g + 1))
                for i in range(NT):
                    last = pe.transpose(pair[k][:, 0, i * P:(i + 1) * P], oT[:, i * P:(i + 1) * P], identf[:])
                last.then_inc(s["oT_ready"], 1)

            def finish(m, b):
                nb = m * B + b
                E = EXPERTS[m]
                k = slot("attnT", nb)
                pe.wait_ge(s["attn_done"], at("attn_done", nb, G))
                turn_tokens(attn, pair[k]).then_inc(s["attnT_ready"], 1)
                k = slot("proj", nb)
                pe.wait_ge(s["attnT_done"], at("attnT_done", nb, 1))
                for i in range(NT):
                    for c in range(C):
                        last = pe.matmul(pair_flat[k][:, i * D:(i + 1) * D], attnT[:, c, i * P:(i + 1) * P],
                                         wo[:, c, :], start=(c == 0), stop=(c == C - 1))
                last.then_inc(s["proj_ready"], 1)
                k = slot("xn2T", nb)
                pe.wait_ge(s["r_norm"], at("r_norm", nb, NT))
                turn_tokens(xn2, pair[k]).then_inc(s["xn2T_ready"], 1)
                pe.wait_ge(s["xn2T_done"], at("xn2T_done", nb, 1))
                for i in range(NT):
                    for c in range(C):
                        last = pe.matmul(ps_logits[:, i * E:(i + 1) * E], xn2T[:, c, i * P:(i + 1) * P],
                                         gate[m][:, c, :], start=(c == 0), stop=(c == C - 1))
                last.then_inc(s["logits_ready"], 1)
                pe.wait_ge(route[m], b * ROUTE[m] + MASKED[m])
                pe.wait_ge(s["mT_done"], at("mT_done", nb, G))
                for i in range(NT):
                    dst = ps_prefix[:, i * E:(i + 1) * E]
                    pe.matmul(dst, tri[:, 0, :], mask_e[:, i, 0:E], start=True, stop=False)
                    for j in range(i):
                        pe.matmul(dst, tri[:, 1, :], mask_e[:, j, 0:E], start=False, stop=False)
                    last = pe.matmul(dst, tri[:, 1, :], before[m][:], start=False, stop=True)
                last.then_inc(s["prefix_ready"], 1)

            def attention(m, b):
                nb = m * B + b
                project(m, b)
                for n in range(8):
                    first_pass(nb, 0, n)
                turn_max(nb, 0)
                for g in range(G):
                    for kb in range(NT):
                        for n in (2 * kb, 2 * kb + 1):
                            second_pass(nb, g, n)
                            if g + 1 < G:
                                first_pass(nb, g + 1, n)
                        if kb >= 1:
                            weigh_values(nb, g, kb - 1)
                    weigh_values(nb, g, NT - 1)
                    if g + 1 < G:
                        turn_max(nb, g + 1)
                    turn_heads(nb, g)
                finish(m, b)

            def plan(m):
                E, T = EXPERTS[m], BLOCKS[m]
                v, t = plan_v[m], plan_t[m]
                pe.wait_ge(route[m], B * ROUTE[m])
                pe.matmul(ps[0:E, 0, 0:1], before[m][:], tri[:, 1, 0:1], start=True, stop=True).then_inc(t, 1)
                pe.wait_ge(v, 2)
                pe.matmul(ps[0:E, 0, 8:9], tri_f[0:E, 1, 0:E], nblk[0:E, 1:2], start=True, stop=True).then_inc(t, 1)
                pe.wait_ge(v, 6)
                pe.matmul(ps[:, 1, 0:T], tri_f[0:E, 2, :], upto[0:E, 0:T], start=True, stop=True)
                pe.matmul(ps[:, 2, 0:T], nblk_row[0:E, :], upto[0:E, 0:T], start=True, stop=True)
                pe.matmul(ps[:, 3, 0:E], nblk_row[0:E, :], tri_f[0:E, 0, 0:E], start=True, stop=True)
                pe.matmul(ps[:, 4, 0:E], nblk_row[0:E, :], tri_f[0:E, 1, 0:E], start=True, stop=True)
                for h in range(-(-T // P)):
                    n = min(P, T - h * P)
                    last = pe.matmul(ps[0:n, 5, 2 * h:2 * h + 2], upto[0:E, h * P:h * P + n], onb[0:E, :],
                                     start=True, stop=True)
                last.then_inc(t, 1)
                pe.wait_ge(blk_in[m], 16 * -(-T // P))
                for h in range(-(-T // P)):
                    n = min(P, T - h * P)
                    last = pe.transpose(ps[:, 6, h * P:h * P + n], ids_f[0:n, h, :], identf[0:n, 0:n])
                last.then_inc(t, 1)

            def experts(m):
                E, T, K2 = EXPERTS[m], BLOCKS[m], HIDDEN[m]
                w = M[m]

                def turn_x(t, tq, r):
                    pe.wait_ge(w[f"gather{r}"], tq * 16 + 16)
                    if not (isinstance(t, int) and t < 2):
                        pe.wait_ge(w["xT_copied"], t - 1)
                    for c in range(C):
                        last = pe.transpose(ps[:, r % 2, c * P:(c + 1) * P], xg[:, r, c * P:(c + 1) * P], identf[:])
                    last.then_inc(w["x_turned"], 1)

                def expert_of(t):
                    if m == 0:
                        return pe.value_load(plan_i[0:1, 0, ds(t, 1)], min_val=0, max_val=E - 1)
                    return pe.value_load(plan_i[0:1, 1, ds(t, 1)], min_val=0, max_val=SLOTS - 1)

                def first_product(t, r):
                    e = expert_of(t)
                    if m == 1:
                        ready = pe.value_load(plan_i[0:1, 0, ds(t, 1)], min_val=0, max_val=E - 1)
                        pe.wait_ge(expert_in, ready * 32 + 32)
                        pe.sem_inc(own_wait, 1)
                    pe.wait_ge(w["xT_copied"], t + 1)
                    if not (isinstance(t, int) and t < 2):
                        pe.wait_ge(w["hid_done"], t - 1)
                    for c in range(C):
                        if m == 0:
                            rhs = w01[:, ds(e, 1), c, :].rearrange("p a n -> p (a n)")
                        else:
                            rhs = ring1[:, ds(e, 1), c * 192:(c + 1) * 192].rearrange("p a n -> p (a n)")
                        last = pe.matmul(ps[:, 2 + r % 2, 0:2 * K2], xgT[:, r % 2, c, :], rhs,
                                         start=(c == 0), stop=(c == C - 1))
                    last.then_inc(w["mm1_ready"], 1)

                def turn_h(t, r):
                    pe.wait_ge(w["hid_done"], t + 1)
                    if not (isinstance(t, int) and t < 2):
                        pe.wait_ge(w["hT_copied"], t - 1)
                    for c in range(-(-K2 // P)):
                        n = min(P, K2 - c * P)
                        last = pe.transpose(ps[0:n, 4 + r % 2, c * P:(c + 1) * P], hid[:, r % 2, c * P:c * P + n],
                                            identf[:])
                    last.then_inc(w["h_turned"], 1)

                def second_product(t, r):
                    e = expert_of(t)
                    pe.wait_ge(w["hT_copied"], t + 1)
                    if not (isinstance(t, int) and t < 2):
                        pe.wait_ge(w["y_copied"], t - 1)
                    if m == 0:
                        for c in range(2):
                            last = pe.matmul(ps[:, 6 + r % 2, 0:D], hidT[:, r % 2, c, :],
                                             wout[:, ds(e, 1), c, :].rearrange("p a n -> p (a n)"),
                                             start=(c == 0), stop=(c == 1))
                    else:
                        last = pe.matmul(ps[:, 6 + r % 2, 0:D], hidT[0:K2, r % 2, 0, :],
                                         ring1[0:K2, ds(e, 1), 384:640].rearrange("p a n -> p (a n)"),
                                         start=True, stop=True)
                    last.then_inc(w["mm2_ready"], 1)

                def body(t, r, tq1, turn=True):
                    turn_h(t - 1, (r - 1) % 4)
                    if turn:
                        turn_x(t + 1, tq1, (r + 1) % 4)
                    first_product(t, r)
                    second_product(t - 1, (r - 1) % 4)

                pe.wait_ge(plan_v[m], PLAN_IDS)
                if m == 0:
                    pe.wait_ge(w0_in, 32)
                turn_x(0, 0, 0)
                turn_x(1, 0, 1)
                first_product(0, 0)
                for t in range(1, 5):
                    body(t, t % 4, (t + 1) // 4)
                with pe.Fori(1, (T - 4) // 4) as q:
                    for r in range(4):
                        body(q * 4 + (r + 1), (r + 1) % 4, q + (1 if r >= 2 else 0))
                for t in range(T - 3, T):
                    body(t, t % 4, (t + 1) // 4, turn=t + 1 < T)
                turn_h(T - 1, (T - 1) % 4)
                second_product(T - 1, (T - 1) % 4)

            pe.wait_ge(const_in, 16 * 9)
            pe.wait_ge(iotas, 14)
            for m in range(2):
                pe.wait_ge(w_in[m], 32)
                with pe.Fori(0, B) as b:
                    attention(m, b)
                plan(m)
                experts(m)

        @block.scalar
        def _(act_):
            def attention(m, b):
                nb = m * B + b
                act_.wait_ge(s["xnT_ready"], at("xnT_ready", nb, 1))
                act_.copy(xnT[:].rearrange("p c t -> p (c t)"), pair_flat[UNIT["xnT"] % 3]).then_inc(s["xnT_done"], 1)
                for i in range(NT):
                    k = UNIT[("qkv", i)] % 3
                    act_.wait_ge(s["qkv_ready"], at("qkv_ready", nb, i + 1))
                    if m == 0:
                        if i >= 2:
                            act_.wait_ge(s["rope_done"], at("rope_done", nb, i - 1))
                        act_.copy(qk_raw[:, i % 2, :], pair[k][:, 0, :]).then_inc(s["qk_copied"], 1)
                    else:
                        act_.copy(qk[:, i, :], pair[k][:, 0, :]).then_inc(s["qk_copied"], 1)
                    act_.wait_ge(s["pv_done"], at("pv_done", nb, 0))
                    act_.copy(values[:, i, :, 0:DH], pair[k][:, 1, 0:D].rearrange("p (h d) -> p h d", h=H))\
                        .then_inc(s["v_copied"], 1)
                for cp in range(2):
                    k = UNIT[("chunk", cp)] % 3
                    act_.wait_ge(s["chunk_ready"], at("chunk_ready", nb, cp + 1))
                    act_.wait_ge(s["qk_stored"], at("qk_stored", nb, 0))
                    act_.wait_ge(s["k_stored"], at("k_stored", nb, 0))
                    act_.copy(parts[:, 0, 2 * cp:2 * cp + 2, :], pair[k]).then_inc(s["part1"], 1)

                def turned_max(g):
                    act_.wait_ge(s["mT_ready"], at("mT_ready", nb, g + 1))
                    if g >= 2:
                        act_.wait_ge(max_in[g - 2], nb * 48 + 48)
                    else:
                        act_.wait_ge(max_in[g + 2], nb * 48)
                    act_.copy(maxT[:, g % 2, :], ps_max).then_inc(s["mT_done"], 1)

                turned_max(0)
                for g in range(G):
                    for n in range(8):
                        kb, p = divmod(n, 2)
                        k = UNIT[("p2", g, n)] % 3
                        act_.wait_ge(s["s2_ready"], at("s2_ready", nb, 8 * g + n + 1))
                        if kb >= 2 or g >= 1:
                            act_.wait_ge(s["pv_done"], at("pv_done", nb, 4 * g + kb - 1))
                        cols = S - kb * P
                        act_.activation(probs[:, kb % 2, 2 * p:2 * p + 2, 0:cols], pair[k][:, :, 0:cols], ACT.Exp,
                                        scale=SCALE).then_inc(s["exp_done"], 1)
                    if g + 1 < G:
                        turned_max(g + 1)
                    act_.wait_ge(s["pv_done"], at("pv_done", nb, 4 * g + 4))
                    if g >= 1:
                        act_.wait_ge(s["oT_ready"], at("oT_ready", nb, g))
                    act_.copy(oT[:], ps_o).then_inc(s["o_copied"], 1)
                act_.wait_ge(s["attnT_ready"], at("attnT_ready", nb, 1))
                act_.copy(attnT[:].rearrange("p c t -> p (c t)"), pair_flat[UNIT["attnT"] % 3])\
                    .then_inc(s["attnT_done"], 1)
                act_.wait_ge(s["xn2T_ready"], at("xn2T_ready", nb, 1))
                act_.copy(xn2T[:].rearrange("p c t -> p (c t)"), pair_flat[UNIT["xn2T"] % 3])\
                    .then_inc(s["xn2T_done"], 1)
                if m == 0:
                    act_.wait_ge(route[0], b * ROUTE[0] + 2 * NT + 2)
                    act_.activation(r_exp[:, :, 0:2], r_prob[:, :, 0:2], ACT.Exp).then_inc(r_exp_done[0], 1)
                else:
                    act_.wait_ge(route[1], b * ROUTE[1] + 1)
                    for i in range(NT):
                        act_.activation(r_exp[:, i, :], ps_logits[:, i * 64:(i + 1) * 64], ACT.Exp,
                                        bias=r_max[:, i:i + 1], accum_out=r_sum[:, i:i + 1]).then_inc(r_exp_done[1], 1)

            def experts(m):
                T, K2 = BLOCKS[m], HIDDEN[m]
                w = M[m]

                def silu(t, r):
                    act_.wait_ge(w["mm1_ready"], t + 1)
                    act_.activation(act[:, r % 2, 0:K2], ps[:, 2 + r % 2, 0:K2], ACT.Silu).then_inc(w["silu_done"], 1)

                def copy_h(t, r):
                    act_.wait_ge(w["h_turned"], t + 1)
                    n = min(P, K2)
                    act_.copy(hidT[0:n, r % 2, 0:-(-K2 // P), :],
                              ps[0:n, 4 + r % 2, 0:-(-K2 // P) * P].rearrange("p (c t) -> p c t", t=P))\
                        .then_inc(w["hT_copied"], 1)

                def copy_y(t, r, th):
                    act_.wait_ge(w["mm2_ready"], t + 1)
                    if not (isinstance(t, int) and t < 2):
                        act_.wait_ge(w[f"y_store{r % 2}"], th * 16)
                    act_.copy(y[:, r % 2, :], ps[:, 6 + r % 2, 0:D]).then_inc(w["y_copied"], 1)
                    act_.wait_ge(w["y_copied"], t + 1)
                    act_.dma_start(y_dram[m][ds(t * P, P), :], y[:, r % 2, :]).then_inc(w[f"y_store{r % 2}"], 16)

                silu(0, 0)
                with act_.Fori(0, (T - 4) // 4) as q:
                    for r in range(4):
                        copy_h(q * 4 + r, r)
                        silu(q * 4 + (r + 1), (r + 1) % 4)
                        copy_y(q * 4 + r, r, q * 2 + r // 2)
                for t in range(T - 3, T):
                    copy_h(t - 1, (t - 1) % 4)
                    silu(t, t % 4)
                    copy_y(t - 1, (t - 1) % 4, (t - 1) // 2)
                copy_h(T - 1, (T - 1) % 4)
                copy_y(T - 1, (T - 1) % 4, (T - 1) // 2)

            for m in range(2):
                act_.wait_ge(ids_zero[m], 16)
                with act_.Fori(0, B) as b:
                    attention(m, b)
                experts(m)

        @block.vector
        def _(v):
            def norm(k, dst, nb, b):
                v.sem_inc(own_wait, 1)
                for i in range(NT):
                    v.bn_stats(stats[k][:, i, :], x[:, ds(NT * b + i, 1), :].rearrange("p a d -> p (a d)"))\
                        .then_inc(s[f"{k}_stats"], 1)
                v.wait_ge(s[f"{k}_stats"], at(f"{k}_stats", nb, NT))
                v.sem_inc(own_wait, 1)
                for i in range(NT):
                    v.bn_aggr(mean_var[k][:, i, :], stats[k][:, i, :]).then_inc(s[f"{k}_aggr"], 1)
                v.wait_ge(s[f"{k}_rstd"], at(f"{k}_rstd", nb, 1))
                for i in range(NT):
                    v.tensor_scalar(dst[:, i, :], x[:, ds(NT * b + i, 1), :].rearrange("p a d -> p (a d)"),
                                    mean_var[k][:, i, 0:1], rstd[k][:, i:i + 1], ALU.subtract, ALU.mult)\
                        .then_inc(s[f"{k}_norm"], 1)

            def maximum(nb, g, n):
                qb, p = divmod(n, 2)
                k = UNIT[("p1", g, n)] % 3
                v.wait_ge(s["s1_ready"], at("s1_ready", nb, 8 * g + n + 1))
                v.tensor_reduce(neg_max[:, g % 2, 2 * p:2 * p + 2, qb:qb + 1], pair[k][:, :, 0:(qb + 1) * P], AX,
                                ALU.max, negate=True).then_inc(s["max_done"], 1)

            def split_max(nb, g):
                src = neg_max[:, g % 2, :, :].rearrange("p h q -> p (h q)")
                parts_, r = max_parts[:, g % 2], max_rest[:, g % 2, :]
                v.wait_ge(s["max_done"], at("max_done", nb, 8 * g + 8))
                v.tensor_copy(parts_[:, 0, :], src).then_inc(s["m_split"], 1)
                v.wait_ge(s["m_split"], at("m_split", nb, 4 * g + 1))
                v.tensor_tensor(r, src, parts_[:, 0, :], ALU.subtract).then_inc(s["m_split"], 1)
                v.wait_ge(s["m_split"], at("m_split", nb, 4 * g + 2))
                v.tensor_copy(parts_[:, 1, :], r).then_inc(s["m_split"], 1)
                v.wait_ge(s["m_split"], at("m_split", nb, 4 * g + 3))
                v.tensor_tensor(parts_[:, 2, :], r, parts_[:, 1, :], ALU.subtract).then_inc(s["m_split"], 1)

            def attention(m, b):
                nb = m * B + b
                norm("a", xn, nb, b)
                if m == 0:
                    for i in range(NT):
                        v.wait_ge(s["qk_copied"], at("qk_copied", nb, i + 1))
                        if i >= 1:
                            v.wait_ge(s["rope_done"], at("rope_done", nb, i))
                        cs = cos[:, i, :].rearrange("p (a d) -> p a d", a=1).to_broadcast([P, 2 * H, DH])
                        v.tensor_tensor(rope[:, 0, :].rearrange("p (h d) -> p h d", h=2 * H),
                                        qk_raw[:, i % 2, :].rearrange("p (h d) -> p h d", h=2 * H), cs, ALU.mult)\
                            .then_inc(s["rope_cos"], 1)
                        v.wait_ge(s["rope_cos"], at("rope_cos", nb, i + 1))
                        v.wait_ge(s["rope_swap"], at("rope_swap", nb, 2 * i + 2))
                        v.tensor_tensor(qk[:, i, :], rope[:, 0, :], rope[:, 1, :], ALU.add).then_inc(s["rope_done"], 1)
                for cp in range(2):
                    k = UNIT[("chunk", cp)] % 3
                    two = lambda a: parts[:, a, 2 * cp:2 * cp + 2, :].rearrange("p c t -> p (c t)")
                    v.wait_ge(s["part1"], at("part1", nb, cp + 1))
                    if cp:
                        v.wait_ge(s["part3"], at("part3", nb, cp))
                    v.tensor_tensor(rest, pair_flat[k], two(0), ALU.subtract).then_inc(s["rest1"], 1)
                    v.wait_ge(s["rest1"], at("rest1", nb, cp + 1))
                    v.tensor_copy(two(1), rest).then_inc(s["part2"], 1)
                    v.wait_ge(s["part2"], at("part2", nb, cp + 1))
                    v.tensor_tensor(two(2), rest, two(1), ALU.subtract).then_inc(s["part3"], 1)
                for n in range(8):
                    maximum(nb, 0, n)
                split_max(nb, 0)
                for g in range(G):
                    if g + 1 < G:
                        for n in range(8):
                            maximum(nb, g + 1, n)
                        split_max(nb, g + 1)
                    k = UNIT[("turn", g)] % 3
                    heads = pair[k][:, 0, :].rearrange("p (i h d) -> p i h d", i=NT, h=HG)
                    v.wait_ge(s["oT_ready"], at("oT_ready", nb, g + 1))
                    v.reciprocal(rec[:].rearrange("p i (h a) -> p i h a", a=1), heads[:, :, :, DH:DH + 1])\
                        .then_inc(s["rec_done"], 1)
                    v.wait_ge(s["rec_done"], at("rec_done", nb, g + 1))
                    v.tensor_tensor(attn[:, :, 64 * g:64 * g + 64].rearrange("p i (h d) -> p i h d", h=HG),
                                    heads[:, :, :, 0:DH],
                                    rec[:].rearrange("p i (h a) -> p i h a", a=1).to_broadcast([P, NT, HG, DH]),
                                    ALU.mult).then_inc(s["attn_done"], 1)
                rows = x[:, ds(NT * b, NT), :].rearrange("p i d -> p (i d)")
                v.wait_ge(s["proj_ready"], at("proj_ready", nb, 1))
                v.tensor_tensor(rows, pair_flat[UNIT["proj"] % 3], rows, ALU.add).then_inc(s["resid_done"], 1)
                v.wait_ge(s["resid_done"], at("resid_done", nb, 1))
                v.wait_ge(s["xn_stored"], at("xn_stored", nb, 0))
                norm("r", xn2, nb, b)
                choose(m, b)

            def choose(m, b):
                E, K = EXPERTS[m], CHOICES[m]
                nb = m * B + b
                done = [0]
                base = b * ROUTE[m]

                def step(ins, wait=True):
                    done[0] += 1
                    ins.then_inc(route[m], 1)
                    if wait:
                        v.wait_ge(route[m], base + done[0])

                def held():
                    v.sem_inc(own_wait, 1)

                logits = ps_logits[:, 0:NT * E].rearrange("p (i e) -> p i e", i=NT)
                col = lambda a: a.rearrange("p (i a) -> p i a", a=1)
                v.wait_ge(s["logits_ready"], at("logits_ready", nb, 1))
                v.wait_ge(scattered[m], b * (16 * NT * K))
                if m == 1:
                    step(v.tensor_reduce(col(r_max[:]), logits, AX, ALU.max, negate=True), wait=False)
                    v.wait_ge(r_exp_done[1], b * NT + NT)
                    step(v.reciprocal(r_inv[:], r_sum[:]))
                    step(v.tensor_tensor(r_prob[:], r_exp[:], col(r_inv[:]).to_broadcast([P, NT, E]), ALU.mult))
                    held()
                    ranked = [r_prob[:, i, :] for i in range(NT)]
                else:
                    held()
                    ranked = [logits[:, i, :] for i in range(NT)]
                for i in range(NT):
                    step(v.max(top[:, i, :], ranked[i]), wait=False)
                v.wait_ge(route[m], base + done[0])
                held()
                for i in range(NT):
                    step(v.max_index(top_i[:, i, :], top[:, i, :], ranked[i]), wait=False)
                if m == 0:
                    step(v.tensor_scalar(r_max[:], top[:, :, 0], -1.0, None, ALU.mult))
                    step(v.tensor_tensor(r_prob[:, :, 0:K], top[:, :, 0:K], col(r_max[:]).to_broadcast([P, NT, K]),
                                         ALU.add))
                    v.wait_ge(r_exp_done[0], b + 1)
                    num = r_exp[:, :, 0:K]
                    step(v.tensor_reduce(col(r_sum[:]), num, AX, ALU.add))
                else:
                    num = top[:, :, 0:K]
                    step(v.tensor_reduce(col(r_sum[:]), num, AX, ALU.add))
                    step(v.tensor_scalar(r_sum[:], r_sum[:], 1e-12, None, ALU.max))
                step(v.reciprocal(r_inv[:], r_sum[:]))
                step(v.tensor_tensor(weight_all[:, ds(NT * b, NT), 0:K], num,
                                     col(r_inv[:]).to_broadcast([P, NT, K]), ALU.mult), wait=False)
                step(v.tensor_copy(chosen[:, :, 0:K], top_i[:, :, 0:K]))
                hot = onehot[:, :, 0:K, 0:E]
                step(v.tensor_tensor(
                    hot, iota_e[:, 0:E].rearrange("p (a b e) -> p a b e", a=1, b=1).to_broadcast([P, NT, K, E]),
                    chosen[:, :, 0:K].rearrange("p i (k a) -> p i k a", a=1).to_broadcast([P, NT, K, E]),
                    ALU.is_equal))
                with nc.allow_low_precision(reason="zeros and ones"):
                    step(v.tensor_reduce(mask_e[:, :, 0:E].rearrange("p i (e a) -> p i e a", a=1),
                                         hot.rearrange("p i k e -> p i e k"), AX, ALU.add), wait=False)
                assert done[0] == MASKED[m]
                v.wait_ge(s["prefix_ready"], at("prefix_ready", nb, 1))
                where = place_e[:, :, 0:E]
                step(v.tensor_tensor(where, ps_prefix[:, 0:NT * E].rearrange("p (i e) -> p i e", i=NT),
                                     base_e[:, 0:E].rearrange("p (a e) -> p a e", a=1).to_broadcast([P, NT, E]),
                                     ALU.add))
                pick = picked[:, 0:NT * K * E].rearrange("p (i k e) -> p i k e", i=NT, k=K)
                step(v.tensor_tensor(pick, hot, where.rearrange("p i (a e) -> p i a e", a=1)
                                     .to_broadcast([P, NT, K, E]), ALU.mult))
                step(v.tensor_reduce(dest_f[:, :, 0:K].rearrange("p i (k a) -> p i k a", a=1), pick, AX, ALU.add))
                step(v.tensor_copy(dest_all[:, ds(NT * b, NT), 0:K], dest_f[:, :, 0:K]), wait=False)
                step(v.tensor_copy(expert_all[:, ds(NT * b, NT), 0:K], chosen[:, :, 0:K]), wait=False)
                step(v.tensor_reduce(tile_sum[:, 0:E].rearrange("p (e a) -> p e a", a=1),
                                     mask_e[:, :, 0:E].rearrange("p i e -> p e i"), AX, ALU.add))
                step(v.tensor_tensor(before[m][:], before[m][:], tile_sum[:, 0:E], ALU.add))
                step(v.tensor_copy(dest[:, :, 0:K], dest_f[:, :, 0:K]), wait=False)
                assert done[0] == ROUTE[m], (done, ROUTE)

            def plan(m):
                E, K, T = EXPERTS[m], CHOICES[m], BLOCKS[m]
                sv, st = plan_v[m], plan_t[m]
                done = [0]

                def step(ins, wait=True):
                    done[0] += 1
                    ins.then_inc(sv, 1)
                    if wait:
                        v.wait_ge(sv, done[0])

                v.wait_ge(st, 1)
                step(v.tensor_scalar(more[0:E, :], iota_j[0:E, :], ps[0:E, 0, 0:1], None, ALU.is_lt))
                v.wait_ge(sv, 1)
                v.tensor_reduce(nblk[0:E, 0:1], more[0:E, :], AX, ALU.add).then_inc(iotas, 1)
                v.wait_ge(iotas, 15 + m)
                step(v.tensor_scalar(nblk[0:E, 1:2], nblk[0:E, 0:1], 1.0, None, ALU.max))
                v.wait_ge(st, 2)
                step(v.tensor_scalar(upto[0:E, 0:T], iota_t[0:E, 0:T], ps[0:E, 0, 8:9], None, ALU.is_ge))
                step(v.tensor_scalar(nblk_row[0:E, :], tri_f[0:E, 2, :], nblk[0:E, 1:2], None, ALU.mult))
                step(v.tensor_copy(onb[0:E, 0:1], tri_f[0:E, 2, 0:1]))
                step(v.tensor_copy(onb[0:E, 1:2], nblk[0:E, 1:2]))
                v.wait_ge(st, 3)
                n = -(-T // P)
                for h in range(n):
                    r = min(P, T - h * P)
                    step(v.tensor_scalar(blk_f[0:r, h, :], ps[0:r, 5, 2 * h:2 * h + 2], 1.0, None, ALU.mult))
                    step(v.tensor_scalar(blk_f[0:r, h, 1:2], iota_p[0:r, h:h + 1], blk_f[0:r, h, 1:2], 31.0,
                                         ALU.subtract, ALU.min))
                    step(v.tensor_scalar(blk_f[0:r, h, 0:1], blk_f[0:r, h, 0:1], float(E - 1), float(TOK // P),
                                         ALU.min, ALU.mult))
                    step(v.tensor_tensor(blk_f[0:r, h, 0:1], blk_f[0:r, h, 0:1], blk_f[0:r, h, 1:2], ALU.add))
                    step(v.tensor_copy(blk_i[0:r, h:h + 1], blk_f[0:r, h, 0:1]))
                for _ in range(2 - n):
                    for _ in range(5):
                        step(v.tensor_copy(corr[:, 0:1], iota_e[:, 0:1]))
                assert done[0] == PLAN_BLOCKS
                step(v.tensor_scalar(plan_f[:, 0:T], ps[:, 1, 0:T], float(E - 1), None, ALU.min))
                step(v.tensor_copy(plan_i[:, 0, 0:T], plan_f[:, 0:T]))
                step(v.tensor_scalar(plan_i[:, 1, 0:T], plan_i[:, 0, 0:T], SLOTS - 1, None, ALU.bitwise_and))
                step(v.tensor_copy(plan_i[:, 2, 0:E], ps[:, 4, 0:E]))
                assert done[0] == PLAN_READY
                step(v.tensor_scalar(corr[:, 0:E], ps[:, 3, 0:E], float(P), None, ALU.mult))
                step(v.tensor_tensor(corr[:, 0:E], corr[:, 0:E], base_e[:, 0:E], ALU.subtract))
                v.wait_ge(st, 4)
                step(v.tensor_copy(ids[:, 0:T], ps[:, 6, 0:T]))
                assert done[0] == PLAN_IDS
                per = min(TILES // 2, 1024 // (K * E))
                n0 = done[0]
                with v.Fori(0, TILES // per) as q:
                    hot = onehot[:].rearrange("p i k e -> p (i k e)")[:, 0:per * K * E].rearrange(
                        "p (i k e) -> p i k e", i=per, k=K)
                    pick = picked[:, 0:per * K * E].rearrange("p (i k e) -> p i k e", i=per, k=K)
                    who = expert_all[:, ds(q * per, per), 0:K]
                    v.wait_ge(sv, q * 4 + n0)
                    v.tensor_tensor(
                        hot, iota_e[:, 0:E].rearrange("p (a b e) -> p a b e", a=1, b=1).to_broadcast([P, per, K, E]),
                        who.rearrange("p i (k a) -> p i k a", a=1).to_broadcast([P, per, K, E]),
                        ALU.is_equal).then_inc(sv, 1)
                    v.wait_ge(sv, q * 4 + (n0 + 1))
                    v.tensor_tensor(pick, hot, corr[:, 0:E].rearrange("p (a b e) -> p a b e", a=1, b=1)
                                    .to_broadcast([P, per, K, E]), ALU.mult).then_inc(sv, 1)
                    v.wait_ge(sv, q * 4 + (n0 + 2))
                    v.sem_inc(own_wait, 1)
                    v.tensor_reduce(expert_all[:, ds(q * per, per), 0:K].rearrange("p i (k a) -> p i k a", a=1),
                                    pick, AX, ALU.add).then_inc(sv, 1)
                    v.wait_ge(sv, q * 4 + (n0 + 3))
                    v.tensor_tensor(slot_all[:, ds(q * per, per), 0:K], expert_all[:, ds(q * per, per), 0:K],
                                    dest_all[:, ds(q * per, per), 0:K], ALU.add).then_inc(sv, 1)

            def experts(m):
                T, K2 = BLOCKS[m], HIDDEN[m]
                w = M[m]

                def copy_x(t, r):
                    v.wait_ge(w["x_turned"], t + 1)
                    v.tensor_copy(xgT[:, r % 2, :, :].rearrange("p c t -> p (c t)"), ps[:, r % 2, 0:D])\
                        .then_inc(w["xT_copied"], 1)

                def gated(t, r):
                    v.wait_ge(w["silu_done"], t + 1)
                    v.tensor_tensor(hid[:, r % 2, 0:K2], ps[:, 2 + r % 2, K2:2 * K2], act[:, r % 2, 0:K2], ALU.mult)\
                        .then_inc(w["hid_done"], 1)

                copy_x(0, 0)
                copy_x(1, 1)
                gated(0, 0)
                with v.Fori(0, (T - 4) // 4) as q:
                    for r in range(4):
                        copy_x(q * 4 + (r + 2), (r + 2) % 4)
                        gated(q * 4 + (r + 1), (r + 1) % 4)
                for t in range(T - 3, T):
                    if t + 1 < T:
                        copy_x(t + 1, (t + 1) % 4)
                    gated(t, t % 4)

            def add_back(m):
                K = CHOICES[m]
                per = RING // K
                used = M[m]["back_used"]
                rounds0 = 0 if m == 0 else TILES * CHOICES[0] // RING
                with v.Fori(0, TILES // per) as q:
                    for r in range(RING):
                        i, k = divmod(r, K)
                        row = x[:, ds(q * per + i, 1), :].rearrange("p a d -> p (a d)")
                        v.wait_ge(back_in[r], (q + rounds0) * 16 + 16)
                        v.wait_ge(used, q * RING + r)
                        v.scalar_tensor_tensor(
                            out=row, in0=back[:, r, :], scalar=weight_all[:, ds(q * per + i, 1), k:k + 1]
                            .rearrange("p a k -> p (a k)"), in1=row, op0=ALU.mult, op1=ALU.add).then_inc(used, 1)

            v.memset(tri_f[:, 2, :], 1.0).then_inc(iotas, 1)
            v.wait_ge(const_in, 16 * 9)
            v.tensor_copy(tri_f[:, 0, :], tri[:, 0, :]).then_inc(iotas, 1)
            v.wait_ge(iotas, 9)
            v.tensor_tensor(tri_f[:, 1, :], tri_f[:, 0, :], identf[:], ALU.add).then_inc(iotas, 1)
            v.memset(k_stack[ROWS:ROWS + 3, :, :], 1.0).then_inc(iotas, 1)
            v.memset(before[0][:], 0.0).then_inc(iotas, 1)
            v.memset(before[1][:], 0.0).then_inc(iotas, 1)
            v.memset(values[:, :, :, DH:DH + 1], 1.0).then_inc(iotas, 1)
            v.wait_ge(iotas, 14)
            v.wait_ge(x_in0, 16)
            v.wait_ge(x_in1, 16)
            for m in range(2):
                with v.Fori(0, B) as b:
                    attention(m, b)
                plan(m)
                experts(m)
                add_back(m)


MASKED = (16, 18)
PLAN_BLOCKS = 16
PLAN_READY = 20
PLAN_IDS = 23


def kernel(**inputs):
    import math
    import ml_dtypes
    import numpy as np
    from concourse import bacc, mybir as mb
    from concourse.bass_utils import run_bass_kernel_spmd

    a = {k: np.asarray(v) for k, v in inputs.items()}
    chunks = lambda w: np.ascontiguousarray(w.reshape(C, P, w.shape[-1]).transpose(1, 0, 2))
    each = lambda w: np.ascontiguousarray(w.reshape(w.shape[0], C, P, w.shape[-1]).transpose(0, 2, 1, 3))
    arrays = {
        "x": a["L0_attn_x"].reshape(TILES, P, D).transpose(1, 0, 2),
        "wqkv0": chunks(a["L0_attn_Wqkv"].T), "wqkv1": chunks(a["L1_attn_Wqkv"]),
        "wo0": chunks(a["L0_attn_WO"].T), "wo1": chunks(a["L1_attn_Wo"]),
        "gate0": chunks(a["L0_ffn_gate_kernel"]), "gate1": chunks(a["L1_ffn_gate_weight"].T),
        "w01_0": each(np.concatenate([a["L0_ffn_wi_0"], a["L0_ffn_wi_1"]], axis=2)).transpose(1, 0, 2, 3),
        "wout_0": each(a["L0_ffn_wo"]).transpose(1, 0, 2, 3),
        "w01_1": each(a["L1_ffn_gate_up_proj"].transpose(0, 2, 1)).reshape(EXPERTS[1], P, C * 2 * HIDDEN[1]),
        "wout_1": a["L1_ffn_down_proj"].transpose(0, 2, 1),
    }
    pos = np.arange(S, dtype=np.float32)
    freqs = np.exp(np.float32(-math.log(10000.0)) * np.arange(0, DH, 2, dtype=np.float32) / np.float32(DH))
    angles = (pos[:, None] * freqs[None, :].astype(np.float32)).astype(np.float32)
    sign = np.tile(np.array([-1.0, 1.0], np.float32), DH // 2)
    by_tile = lambda t: t.reshape(NT, P, DH).transpose(1, 0, 2)
    arrays["cos"] = by_tile(np.repeat(np.cos(angles), 2, axis=1).astype(np.float32))
    arrays["sin"] = by_tile((np.repeat(np.sin(angles), 2, axis=1) * sign).astype(np.float32))
    row, col = np.arange(P)[:, None], np.arange(P)[None, :]
    arrays["identf"] = np.eye(P, dtype=np.float32)
    arrays["identb"] = np.eye(P, dtype=np.float32).astype(ml_dtypes.bfloat16)
    arrays["masks"] = np.stack([np.where(col > row, -1e30, 0.0), np.where(row > col, -1e30, 0.0)], axis=1)\
        .astype(ml_dtypes.bfloat16)
    arrays["tri"] = np.stack([(row < col).astype(np.float32), np.ones((P, P), np.float32)], axis=1)\
        .astype(ml_dtypes.bfloat16)
    arrays["token"] = (np.arange(TILES)[None, :] * P + row).astype(np.float32)
    arrays = {f"in_{k}": np.ascontiguousarray(v) for k, v in arrays.items()}

    nc = bacc.Bacc("TRN2", target_bir_lowering=False, num_devices=1)
    t = {k[3:]: nc.dram_tensor(k, v.shape, mb.dt.from_np(v.dtype), kind="ExternalInput").ap()
         for k, v in arrays.items()}
    out = nc.dram_tensor("out", (P, TILES, D), mb.dt.float32, kind="ExternalOutput").ap()
    two = lambda k: [t[f"{k}0"], t[f"{k}1"]]
    two_moe_layers(nc, t["x"], two("wqkv"), two("wo"), two("gate"), two("w01_"), two("wout_"), t["cos"], t["sin"],
                   t["identf"], t["identb"], t["masks"], t["tri"], t["token"], out)
    r = run_bass_kernel_spmd(nc, [arrays], core_ids=[0])
    return np.ascontiguousarray(r.results[0]["out"].transpose(1, 0, 2)).reshape(B, S, D)
```

```python
from contextlib import ExitStack

import concourse.bass as bass
from concourse import mybir

ALU = mybir.AluOpType
ACT = mybir.ActivationFunctionType
F32 = mybir.dt.float32
BF16 = mybir.dt.bfloat16
U32 = mybir.dt.uint32
I32 = mybir.dt.int32
AX = mybir.AxisListType.X
ds = bass.ds

P = 128
B, S, D = 8, 512, 256
H, DH = 16, 16
NT = S // P
TILES = B * NT
TOK = B * S
C = D // P
HG = 4
G = H // HG
HV = 32
SCALE = float(DH) ** -0.5
EPS = 1e-5
ROWS = DH * 6
EXPERTS, CHOICES, HIDDEN = (8, 64), (2, 4), (256, 96)


def blocks(layer):
    e, k = EXPERTS[layer], CHOICES[layer]
    return -(-(TOK * k // P + e - 1) // 8) * 8


BLOCKS = (blocks(0), blocks(1))
SLOTS = 8
RING = 8

PER = dict(a_stats=4, a_aggr=4, a_eps=1, a_rstd=1, a_norm=4, r_stats=4, r_aggr=4, r_eps=1, r_rstd=1,
           r_norm=4, xnT_ready=1, xnT_done=1, qkv_ready=4, qk_copied=4, v_copied=4, chunk_ready=2,
           part1=2, rest1=2, part2=2, part3=2, s1_ready=32, max_done=32, s2_ready=32, exp_done=32,
           pv_done=16, m_split=16, mT_ready=4, mT_done=4, o_copied=4, oT_ready=4, rec_done=4,
           attn_done=4, attnT_ready=1, attnT_done=1, proj_ready=1, resid_done=1, xn2T_ready=1,
           xn2T_done=1, logits_ready=1, prefix_ready=1, tok_ready=1, qk_stored=48, k_stored=48,
           xn_stored=16, rope_cos=4, rope_swap=8, rope_done=4)

LAST, NOW, NEXT = -1, 0, 1


def step_units():
    def passes(g1, g2, batch2, extra=None):
        p1 = [(("p1", g1, n), "max_done", 8 * g1 + n + 1, NOW) for n in range(8)]
        u = p1[0:2]
        for n in range(8):
            u.append((("p2", g2, n), "exp_done", 8 * g2 + n + 1, batch2))
            u += p1[n + 2:n + 3]
            if extra and n == 1:
                u.append(extra)
        return u
    turn = lambda g, batch: (("turn", g), "attn_done", g + 1, batch)
    qkv = lambda i: (("qkv", i), "v_copied", i + 1, NEXT)
    u = passes(0, 3, LAST)
    u += [turn(3, LAST), ("xnT", "xnT_done", 1, NEXT), qkv(0), ("attnT", "attnT_done", 1, LAST), qkv(1)]
    u += passes(1, 0, NOW, extra=("proj", "resid_done", 1, LAST))
    u += [turn(0, NOW), qkv(2), qkv(3), ("xn2T", "xn2T_done", 1, LAST)]
    u += passes(2, 1, NOW)
    u += [turn(1, NOW)] + [(("chunk", i), "rest1", i + 1, NEXT) for i in range(2)]
    u += passes(3, 2, NOW)
    u += [turn(2, NOW)]
    assert len(u) % 3 == 0
    return u


UNITS = step_units()
UNIT = {name: n for n, (name, *_) in enumerate(UNITS)}


def held_before(name, has, had):
    n = UNIT[name]
    for k in range(n - 3, -1, -3):
        _, done, count, batch = UNITS[k]
        if batch in has:
            return done, count, batch
    for k in range(len(UNITS) - 3 + n % 3, -1, -3):
        _, done, count, batch = UNITS[k]
        if batch in had:
            return done, count, batch - 1
    return None


def two_moe_layers(nc, x_in, wqkv_in, wo_in, gate_in, w01_in, wout_in, cos_in, sin_in, identf_in, identb_in,
                   masks_in, tri_in, token_in, out):
    ctx = ExitStack()
    with ctx:
        def sb(name, shape, dt=F32):
            return ctx.enter_context(nc.sbuf_tensor(name, shape, dt))

        def sem(name):
            return ctx.enter_context(nc.semaphore(name))

        def dram(name, shape, dt=F32):
            return nc.dram_tensor(name, shape, dt, kind="Internal").ap()

        parts_dram = dram("parts_dram", (2, 3, DH, H, S), BF16)
        xn_dram = dram("xn_dram", (TOK, D))
        id_dram = [dram(f"id_dram{m}", (EXPERTS[m] * TOK, 1)) for m in range(2)]
        y_dram = [dram(f"y_dram{m}", (BLOCKS[m] * P, D)) for m in range(2)]

        x = sb("x", [P, TILES, D])
        wqkv = sb("wqkv", [P, C, 3 * D])
        wo = sb("wo", [P, C, D])
        gate = [sb(f"gate{m}", [P, C, EXPERTS[m]]) for m in range(2)]
        w01 = sb("w01", [P, EXPERTS[0], C, 2 * HIDDEN[0]])
        ring1 = w01[:, :, :, :].rearrange("p e c n -> p (e c n)")[:, 0:SLOTS * 640].rearrange(
            "p (s n) -> p s n", s=SLOTS)
        q_stack = sb("q_stack", [P, H, S], BF16)
        k_stack = sb("k_stack", [P, H, S], BF16)
        values = sb("values", [P, 2, NT, H, HV])
        probs = sb("probs", [P, 2, HG, S])
        wout = probs[:, :, :, :].rearrange("p a h s -> p (a h s)").rearrange("p (e c n) -> p e c n", e=8, c=C)
        xn = sb("xn", [P, NT, D])
        xnT = sb("xnT", [P, C, S])
        qk = sb("qk", [P, NT, 2 * D])
        oT = sb("oT", [P, S])
        attn = sb("attn", [P, NT, D])
        attnT = sb("attnT", [P, C, S])
        xn2 = xn
        xn2T = attnT
        work = sb("work", [P, 6144])
        parts = work[:, 0:3072].bitcast(BF16).rearrange("p (a c s) -> p a c s", a=3, c=4)
        qk_raw = work[:, 3072:4096].rearrange("p (a n) -> p a n", a=2)
        rest = work[:, 4096:6144].rearrange("p (a n) -> p a n", a=2)
        rope = rest[:, 1, :].rearrange("p (a n) -> p a n", a=2)
        xg = work[:, 0:1024].rearrange("p (r n) -> p r n", r=4)
        xgT = work[:, 1024:1536].rearrange("p (r c t) -> p r c t", r=2, c=C)
        act = work[:, 1536:2048].rearrange("p (r n) -> p r n", r=2)
        hid = work[:, 2048:2560].rearrange("p (r n) -> p r n", r=2)
        hidT = work[:, 2560:3072].rearrange("p (r c t) -> p r c t", r=2, c=C)
        y = work[:, 3072:3584].rearrange("p (r n) -> p r n", r=2)
        back = work[:, 3584:3584 + RING * D].rearrange("p (r n) -> p r n", r=RING)

        cos = sb("cos", [P, NT, DH])
        sin = sb("sin", [P, NT, DH])
        identf = sb("identf", [P, P])
        identb = sb("identb", [P, P], BF16)
        masks = sb("masks", [P, 2, P], BF16)
        tri = sb("tri", [P, 2, P], BF16)
        tri_f = sb("tri_f", [P, 3, P])
        token = sb("token", [P, TILES])
        iota_e = sb("iota_e", [P, 64])
        base_e = sb("base_e", [P, 64])
        iota_t = sb("iota_t", [P, 192])
        iota_j = sb("iota_j", [P, 32])
        iota_p = sb("iota_p", [P, 2])
        half = sb("half", [P, NT])
        zeros = probs[:, 0, :, :].rearrange("p h s -> p (h s)")
        ids_f = work[:, 5824:6080].rearrange("p (a n) -> p a n", a=2)
        stats = {k: sb(f"{k}_st", [P, NT, 6]) for k in "ar"}
        mean_var = {k: sb(f"{k}_mv", [P, NT, 2]) for k in "ar"}
        var_eps = {k: sb(f"{k}_ve", [P, NT]) for k in "ar"}
        rstd = {k: sb(f"{k}_rs", [P, NT]) for k in "ar"}
        neg_max = sb("neg_max", [P, 2, HG, NT])
        max_rest = sb("max_rest", [P, 2, HG * NT])
        max_parts = sb("max_parts", [P, 2, 3, HG * NT], BF16)
        maxT = sb("maxT", [3 * HG * NT, 2, P], BF16)
        rec = sb("rec", [P, NT, HG])
        r_max = sb("r_max", [P, NT])
        r_exp = sb("r_exp", [P, NT, 64])
        r_sum = sb("r_sum", [P, NT])
        r_inv = sb("r_inv", [P, NT])
        r_prob = sb("r_prob", [P, NT, 64])
        top = sb("top", [P, NT, 8])
        top_i = sb("top_i", [P, NT, 8], U32)
        chosen = sb("chosen", [P, NT, 4])
        onehot = sb("onehot", [P, NT, 4, 64], BF16)
        picked = work[:, 3072:4096]
        mask_e = sb("mask_e", [P, NT, 64], BF16)
        tile_sum = sb("tile_sum", [P, 64])
        before = [sb(f"before{m}", [P, EXPERTS[m]], BF16) for m in range(2)]
        place_e = sb("place_e", [P, NT, 64])
        dest_f = sb("dest_f", [P, NT, 4])
        dest = sb("dest", [P, NT, 4], U32)
        token_now = sb("token_now", [P, NT])
        dest_all = sb("dest_all", [P, TILES, 4])
        expert_all = sb("expert_all", [P, TILES, 4])
        weight_all = sb("weight_all", [P, TILES, 4])
        slot_all = sb("slot_all", [P, TILES, 4], U32)
        nblk = sb("nblk", [64, 4])
        more = sb("more", [64, 32])
        upto = sb("upto", [64, 192])
        nblk_row = sb("nblk_row", [64, P])
        onb = sb("onb", [64, 2])
        plan_f = work[:, 5632:5824]
        plan_i = sb("plan_i", [P, 3, 192], I32)
        corr = sb("corr", [P, 64])
        blk_f = sb("blk_f", [P, 2, 2])
        blk_i = sb("blk_i", [P, 2], U32)
        ids = sb("ids", [P, 192], U32)
        ids_now = sb("ids_now", [P, 2, 4], U32)
        slots_now = sb("slots_now", [P, 2, RING], U32)

        ps = ctx.enter_context(nc.psum_tensor("ps", [P, 8, 512], F32))
        pair = [ps[:, 2 * i:2 * i + 2, :] for i in range(3)]
        pair_flat = [v.rearrange("p a n -> p (a n)") for v in pair]
        ps_o = ps[:, 6, :]
        ps_logits = ps[:, 7, 0:256]
        ps_prefix = ps_logits
        ps_max = ps[0:48, 7, 256:320].bitcast(BF16)

        s = {k: sem(k) for k in PER}
        const_in = sem("const_in")
        x_in0, x_in1 = sem("x_in0"), sem("x_in1")
        w_in = [sem(f"w_in{m}") for m in range(2)]
        w0_in = sem("w0_in")
        iotas = sem("iotas")
        zeroed = sem("zeroed")
        own_wait = sem("own_wait")
        stack_in = [sem(f"stack_in{g}") for g in range(G)]
        max_in = [sem(f"max_in{g}") for g in range(G)]
        ids_zero = [sem(f"ids_zero{m}") for m in range(2)]
        route = [sem(f"route{m}") for m in range(2)]
        r_exp_done = [sem(f"r_exp_done{m}") for m in range(2)]
        scattered = [sem(f"scattered{m}") for m in range(2)]
        plan_v = [sem(f"plan_v{m}") for m in range(2)]
        plan_t = [sem(f"plan_t{m}") for m in range(2)]
        blk_in = [sem(f"blk_in{m}") for m in range(2)]
        M = [{k: sem(f"{k}{m}") for k in (
            "gather0", "gather1", "gather2", "gather3", "x_turned", "xT_copied", "mm1_ready", "silu_done",
            "hid_done", "h_turned", "hT_copied", "mm2_ready", "y_copied", "y_store0", "y_store1",
            "ids_copied", "slots_copied", "back_used")} for m in range(2)]
        back_in = [sem(f"back_in{r}") for r in range(RING)]
        expert_in = sem("expert_in")
        out_sem = sem("out_sem")
        ROUTE = (24, 26)

        def at(name, nb, n):
            return nb * PER[name] + n

        def after_first(engine, semaphore, count):
            if not isinstance(count, int) or count > 0:
                engine.wait_ge(semaphore, count)

        HAD = {(NEXT,): (), (NOW, NEXT): (NEXT,), (LAST, NOW, NEXT): (LAST, NOW, NEXT),
               (LAST, NOW): (LAST, NOW, NEXT), (LAST,): (LAST, NOW)}
        block = ctx.enter_context(nc.Block())

        @block.sync
        def _(sp):
            sp.dma_start(identf[:], identf_in).then_inc(const_in, 16)
            sp.dma_start(x[:, 0:NT, :], x_in[:, 0:NT, :]).then_inc(x_in0, 16)
            sp.dma_start(wqkv[:], wqkv_in[0]).then_inc(w_in[0], 16)
            for dst, src in ((identb, identb_in), (masks, masks_in), (cos, cos_in), (sin, sin_in),
                             (tri, tri_in), (token, token_in), (gate[0], gate_in[0]), (gate[1], gate_in[1])):
                sp.dma_start(dst[:], src).then_inc(const_in, 16)
            sp.dma_start(wo[:], wo_in[0]).then_inc(w_in[0], 16)
            sp.dma_start(x[:, NT:TILES, :], x_in[:, NT:TILES, :]).then_inc(x_in1, 16)
            sp.dma_start(w01[:], w01_in[0]).then_inc(w0_in, 16)
            sp.wait_ge(zeroed, 1)
            for m in range(2):
                n = EXPERTS[m] * TOK // P
                sp.dma_start(id_dram[m].rearrange("(p a) b -> p (a b)", p=P), zeros[:, 0:n]).then_inc(ids_zero[m], 16)

            def store_parts(nb):
                for cp, stored in ((0, "qk_stored"), (1, "k_stored")):
                    sp.wait_ge(s["part3"], at("part3", nb, cp + 1))
                    sp.sem_inc(own_wait, 1)
                    sp.wait_ge(s["part2"], at("part2", nb, cp + 1))
                    sp.sem_inc(own_wait, 1)
                    if cp == 0:
                        after_first(sp, stack_in[G - 1], nb * 96)
                    for a in range(3):
                        sp.dma_start(parts_dram[cp, a].rearrange("r (c h) s -> h r c s", c=2),
                                     parts[:, a, 2 * cp:2 * cp + 2, :]).then_inc(s[stored], 16)
                sp.wait_ge(s["qk_stored"], at("qk_stored", nb, 48))
                sp.wait_ge(s["k_stored"], at("k_stored", nb, 48))
                sp.sem_inc(own_wait, 1)

            def load_stack(nb, g):
                after_first(sp, s["s2_ready"], at("s2_ready", nb - 1, 8 * g + 8))
                heads = slice(HG * g, HG * g + HG)
                for n in range(3):
                    rows = slice(DH * (0, 3, 5)[n], DH * (3, 5, 6)[n])
                    sp.dma_start(q_stack[rows, heads, :],
                                 parts_dram[0, 0:3 - n, :, heads, :].rearrange("a r h s -> (a r) h s"))\
                        .then_inc(stack_in[g], 16)
                    sp.dma_start(k_stack[rows, heads, :],
                                 parts_dram[1, n:n + 1, :, heads, :].to_broadcast([3 - n, DH, HG, S]))\
                        .then_inc(stack_in[g], 16)

            def step(m, b, has):
                nb = m * B + b
                if NOW in has:
                    load_stack(nb, 3)
                if LAST in has:
                    sp.wait_ge(s["r_norm"], at("r_norm", nb - 1, NT))
                    sp.sem_inc(own_wait, 1)
                    sp.dma_start(xn_dram.rearrange("(i p) d -> p i d", p=P)[:, ds(NT * (b - 1), NT), :], xn2[:])\
                      .then_inc(s["xn_stored"], 16)
                if NEXT in has:
                    store_parts(nb + 1)
                    for g in range(3):
                        load_stack(nb + 1, g)

            for m in range(2):
                step(m, -1, (NEXT,))
                step(m, 0, (NOW, NEXT))
                with sp.Fori(1, B - 1) as b:
                    step(m, b, (LAST, NOW, NEXT))
                step(m, B - 1, (LAST, NOW))
                step(m, B, (LAST,))
                if m == 0:
                    sp.wait_ge(s["pv_done"], at("pv_done", B, 0))
                    sp.dma_start(wout, wout_in[0]).then_inc(w0_in, 16)
                    sp.wait_ge(s["proj_ready"], at("proj_ready", B, 0))
                    sp.dma_start(wqkv[:], wqkv_in[1]).then_inc(w_in[1], 16)
                    sp.dma_start(wo[:], wo_in[1]).then_inc(w_in[1], 16)
                    sp.wait_ge(M[0]["mm1_ready"], BLOCKS[0])
                    sp.nop()
                else:
                    def load_expert(e, slot):
                        sp.dma_start(ring1[:, slot, 0:384], w01_in[1][e]).then_inc(expert_in, 16)
                        sp.dma_start(ring1[0:HIDDEN[1], slot, 384:640], wout_in[1][e]).then_inc(expert_in, 16)

                    for e in range(SLOTS):
                        load_expert(e, e)
                        sp.wait_ge(expert_in, 32 * (e + 1))
                    sp.wait_ge(plan_v[1], PLAN_READY)
                    with sp.Fori(1, EXPERTS[1] // SLOTS) as q:
                        for r in range(SLOTS):
                            done = sp.value_load(plan_i[0:1, 2, ds(q * SLOTS + (r - SLOTS), 1)],
                                                 min_val=0, max_val=BLOCKS[1])
                            sp.wait_ge(M[1]["mm2_ready"], done)
                            sp.sem_inc(own_wait, 1)
                            e = q * SLOTS + r
                            sp.dma_start(ring1[:, r, 0:384],
                                         w01_in[1][ds(e, 1)].rearrange("a p n -> (a p) n")).then_inc(expert_in, 16)
                            sp.dma_start(ring1[0:HIDDEN[1], r, 384:640],
                                         wout_in[1][ds(e, 1)].rearrange("a p n -> (a p) n")).then_inc(expert_in, 16)
                            sp.wait_ge(expert_in, 32 * (e + 1))
                            sp.sem_inc(own_wait, 1)
                    per = RING // CHOICES[1]
                    with sp.Fori(0, TILES // per) as q:
                        sp.wait_ge(M[1]["back_used"], (q + 1) * RING)
                        sp.sem_inc(own_wait, 1)
                        sp.dma_start(out[:, ds(q * per, per), :], x[:, ds(q * per, per), :]).then_inc(out_sem, 16)
                    sp.wait_ge(out_sem, 16 * TILES // per)

        @block.gpsimd
        def _(pool):
            pool.memset(zeros, 0.0).then_inc(zeroed, 1)
            pool.memset(half[:], -0.5).then_inc(iotas, 1)
            imprecise = dict(allow_small_or_imprecise_dtypes=True)
            pool.iota(iota_e[:], pattern=[[1, 64]], base=0, channel_multiplier=0, **imprecise).then_inc(iotas, 1)
            pool.iota(base_e[:], pattern=[[TOK, 64]], base=0, channel_multiplier=0, **imprecise).then_inc(iotas, 1)
            pool.iota(iota_t[:], pattern=[[1, 192]], base=0, channel_multiplier=0, **imprecise).then_inc(iotas, 1)
            pool.iota(iota_j[:], pattern=[[P, 32]], base=0, channel_multiplier=0, **imprecise).then_inc(iotas, 1)
            pool.iota(iota_p[:], pattern=[[P, 2]], base=0, channel_multiplier=1, **imprecise).then_inc(iotas, 1)
            pool.memset(values[:, :, :, :, DH:HV], 0.0).then_inc(iotas, 1)

            def rstd_of(k, nb):
                pool.wait_ge(s[f"{k}_aggr"], at(f"{k}_aggr", nb, NT))
                pool.sem_inc(own_wait, 1)
                pool.tensor_scalar(var_eps[k][:], mean_var[k][:, :, 1], EPS, None, ALU.add).then_inc(s[f"{k}_eps"], 1)
                pool.wait_ge(s[f"{k}_eps"], at(f"{k}_eps", nb, 1))
                pool.tensor_tensor(rstd[k][:], var_eps[k][:], half[:], ALU.pow).then_inc(s[f"{k}_rstd"], 1)

            def rotate(nb, i):
                pool.wait_ge(s["qk_copied"], at("qk_copied", nb, i + 1))
                if i >= 1:
                    pool.wait_ge(s["rope_done"], at("rope_done", nb, i))
                cs = cos[:, i, :].rearrange("p (a d) -> p a d", a=1).to_broadcast([P, 2 * H, DH])
                pool.tensor_tensor(rope[:, 0, :].rearrange("p (h d) -> p h d", h=2 * H),
                                   qk_raw[:, i % 2, :].rearrange("p (h d) -> p h d", h=2 * H), cs, ALU.mult)\
                    .then_inc(s["rope_cos"], 1)
                raw = qk_raw[:, i % 2, :].rearrange("p (h j e) -> p h j e", h=2 * H, e=2)
                swap = rope[:, 1, :].rearrange("p (h j e) -> p h j e", h=2 * H, e=2)
                for e in range(2):
                    sn = sin[:, i, e::2].rearrange("p (a j) -> p a j", a=1).to_broadcast([P, 2 * H, DH // 2])
                    pool.tensor_tensor(swap[:, :, :, e], raw[:, :, :, 1 - e], sn, ALU.mult)\
                        .then_inc(s["rope_swap"], 1)

            def third_part(nb, cp):
                two = lambda a: parts[:, a, 2 * cp:2 * cp + 2, :].rearrange("p c t -> p (c t)")
                pool.wait_ge(s["part2"], at("part2", nb, cp + 1))
                pool.tensor_tensor(two(2), rest[:, cp, :], two(1), ALU.subtract).then_inc(s["part3"], 1)

            def scatter(m, b):
                nb = m * B + b
                after_first(pool, scattered[m], b * (16 * NT * CHOICES[m]))
                pool.sem_inc(own_wait, 1)
                pool.tensor_copy(token_now[:], token[:, ds(NT * b, NT)]).then_inc(s["tok_ready"], 1)
                pool.wait_ge(s["tok_ready"], at("tok_ready", nb, 1))
                pool.sem_inc(own_wait, 1)
                pool.wait_ge(route[m], b * ROUTE[m] + ROUTE[m])
                pool.sem_inc(own_wait, 1)
                for i in range(NT):
                    for k in range(CHOICES[m]):
                        pool.indirect_dma_start(
                            id_dram[m], bass.IndirectOffsetOnAxis(ap=dest[:, i, k:k + 1], axis=0),
                            token_now[:, i:i + 1], None).then_inc(scattered[m], 16)

            def step(m, b, has):
                nb = m * B + b
                if NEXT in has:
                    rstd_of("a", nb + 1)
                    if m == 0:
                        rotate(nb + 1, 0)
                        rotate(nb + 1, 1)
                if LAST in has:
                    rstd_of("r", nb - 1)
                if NEXT in has:
                    if m == 0:
                        rotate(nb + 1, 2)
                        rotate(nb + 1, 3)
                    third_part(nb + 1, 0)
                    third_part(nb + 1, 1)
                if LAST in has:
                    scatter(m, b - 1)

            def find_blocks(m):
                pool.wait_ge(scattered[m], B * 16 * NT * CHOICES[m])
                pool.wait_ge(plan_v[m], PLAN_BLOCKS)
                table = id_dram[m].rearrange("(r c) b -> r (c b)", c=P)
                for h in range(-(-BLOCKS[m] // P)):
                    n = min(P, BLOCKS[m] - h * P)
                    pool.indirect_dma_start(ids_f[0:n, h, :], None, table,
                                            bass.IndirectOffsetOnAxis(ap=blk_i[0:n, h:h + 1], axis=0))\
                        .then_inc(blk_in[m], 16)

            def gathers(m, q):
                for j in range(2):
                    t0 = q * 8 + 4 * j
                    first = isinstance(q, int)
                    if not first:
                        pool.wait_ge(M[m]["xT_copied"], t0 - 4)
                        pool.sem_inc(own_wait, 1)
                    pool.tensor_copy(ids_now[:, j, :], ids[:, ds(t0, 4)]).then_inc(M[m]["ids_copied"], 1)
                    pool.wait_ge(M[m]["ids_copied"], q * 2 + j + 1)
                    pool.sem_inc(own_wait, 1)
                    for r in range(4):
                        if not (first and j == 0):
                            pool.wait_ge(M[m]["xT_copied"], t0 + (r - 3))
                            pool.sem_inc(own_wait, 1)
                        pool.indirect_dma_start(xg[:, r, :], None, xn_dram,
                                                bass.IndirectOffsetOnAxis(ap=ids_now[:, j, r:r + 1], axis=0))\
                            .then_inc(M[m][f"gather{r}"], 16)

            def gathers_back(m, q):
                flat = slot_all[:, :, 0:CHOICES[m]].rearrange("p i k -> p (i k)") if CHOICES[m] == 4 else None
                for j in range(2):
                    rnd = q * 2 + j
                    if not (isinstance(q, int) and j == 0):
                        pool.wait_ge(M[m]["back_used"], rnd * RING - RING + 1)
                        pool.sem_inc(own_wait, 1)
                    per = RING // CHOICES[m]
                    pool.tensor_copy(slots_now[:, j, :].rearrange("p (i k) -> p i k", i=per),
                                     slot_all[:, ds(rnd * per, per), 0:CHOICES[m]]).then_inc(M[m]["slots_copied"], 1)
                    pool.wait_ge(M[m]["slots_copied"], rnd + 1)
                    pool.sem_inc(own_wait, 1)
                    for r in range(RING):
                        if not (isinstance(q, int) and j == 0):
                            pool.wait_ge(M[m]["back_used"], rnd * RING + (r - RING + 1))
                            pool.sem_inc(own_wait, 1)
                        pool.indirect_dma_start(back[:, r, :], None, y_dram[m],
                                                bass.IndirectOffsetOnAxis(ap=slots_now[:, j, r:r + 1], axis=0))\
                            .then_inc(back_in[r], 16)

            pool.wait_ge(const_in, 16 * 9)
            pool.wait_ge(iotas, 14)
            for m in range(2):
                pool.wait_ge(ids_zero[m], 16)
                step(m, -1, (NEXT,))
                step(m, 0, (NOW, NEXT))
                with pool.Fori(1, B - 1) as b:
                    step(m, b, (LAST, NOW, NEXT))
                step(m, B - 1, (LAST, NOW))
                step(m, B, (LAST,))
                find_blocks(m)
                pool.wait_ge(plan_v[m], PLAN_IDS)
                pool.wait_ge(s["xn_stored"], 16 * B * (m + 1))
                gathers(m, 0)
                with pool.Fori(1, BLOCKS[m] // 8) as q:
                    gathers(m, q)
                for r in range(2):
                    pool.wait_ge(M[m][f"y_store{r}"], 16 * (BLOCKS[m] // 2))
                gathers_back(m, 0)
                with pool.Fori(1, TILES * CHOICES[m] // RING // 2) as q:
                    gathers_back(m, q)

        @block.tensor
        def _(pe):
            def slot(name, nb, has):
                held = held_before(name, has, HAD[has])
                if held:
                    done, count, batch = held
                    pe.wait_ge(s[done], at(done, nb + batch, count))
                return UNIT[name] % 3

            def turn_tokens(src, dst):
                for c in range(C):
                    for i in range(NT):
                        last = pe.transpose(dst[:, c, i * P:(i + 1) * P], src[:, i, c * P:(c + 1) * P], identf[:])
                return last

            def turn_next(nb, has):
                k = slot("xnT", nb, has)
                pe.wait_ge(s["a_norm"], at("a_norm", nb + 1, NT))
                turn_tokens(xn, pair[k]).then_inc(s["xnT_ready"], 1)

            def project(nb, i, has):
                k = slot(("qkv", i), nb, has)
                if i == 0:
                    pe.wait_ge(s["xnT_done"], at("xnT_done", nb + 1, 1))
                for c in range(C):
                    lhs = xnT[:, c, i * P:(i + 1) * P]
                    pe.matmul(pair[k][:, 0, :], lhs, wqkv[:, c, 0:2 * D], start=(c == 0), stop=(c == C - 1))
                    last = pe.matmul(pair[k][:, 1, 0:D], lhs, wqkv[:, c, 2 * D:3 * D],
                                     start=(c == 0), stop=(c == C - 1))
                last.then_inc(s["qkv_ready"], 1)

            def turn_chunk(m, nb, cp, has):
                k = slot(("chunk", cp), nb, has)
                if cp == 0:
                    done = "rope_done" if m == 0 else "qk_copied"
                    pe.wait_ge(s[done], at(done, nb + 1, NT))
                for half_ in range(2):
                    for i in range(NT):
                        c0 = (2 * cp + half_) * P
                        last = pe.transpose(pair[k][:, half_, i * P:(i + 1) * P], qk[:, i, c0:c0 + P], identf[:])
                last.then_inc(s["chunk_ready"], 1)

            def first_pass(nb, g, n, has):
                qb, p = divmod(n, 2)
                k = slot(("p1", g, n), nb, has)
                if n == 0:
                    pe.wait_ge(stack_in[g], nb * 96 + 96)
                for j in range(2):
                    h = HG * g + 2 * p + j
                    pe.matmul(pair[k][:, j, 0:(qb + 1) * P], q_stack[0:ROWS, h, qb * P:(qb + 1) * P],
                              k_stack[0:ROWS, h, 0:(qb + 1) * P], start=True, stop=False)
                    last = pe.matmul(pair[k][:, j, qb * P:(qb + 1) * P], identb[:], masks[:, 0, :],
                                     start=False, stop=True)
                last.then_inc(s["s1_ready"], 1)

            def turn_max(nb, g):
                pe.wait_ge(s["m_split"], at("m_split", nb, 4 * g + 4))
                after_first(pe, s["mT_done"], at("mT_done", nb, g))
                pe.sem_inc(own_wait, 1)
                pe.transpose(ps_max, max_parts[:, g % 2, :, :].rearrange("p a n -> p (a n)"), identb[:])\
                    .then_inc(s["mT_ready"], 1)

            def second_pass(nb, batch, g, n, has):
                kb, p = divmod(n, 2)
                k = slot(("p2", g, n), nb, has)
                if n == 0:
                    pe.wait_ge(max_in[g], (nb + batch) * 16 + 16)
                cols = S - kb * P
                for j in range(2):
                    h = HG * g + 2 * p + j
                    pe.matmul(pair[k][:, j, 0:cols], k_stack[0:ROWS + 3, h, kb * P:(kb + 1) * P],
                              q_stack[0:ROWS + 3, h, kb * P:S], start=True, stop=False)
                    last = pe.matmul(pair[k][:, j, 0:P], identb[:], masks[:, 1, :], start=False, stop=True)
                last.then_inc(s["s2_ready"], 1)

            def weigh_values(nb, par, g, kb):
                pe.wait_ge(s["exp_done"], at("exp_done", nb, 8 * g + 2 * kb + 2))
                if kb == 0:
                    after_first(pe, s["o_copied"], at("o_copied", nb, g))
                cols = S - kb * P
                for j in range(HG):
                    last = pe.matmul(ps_o[HV * j:HV * j + HV, kb * P:S], values[:, par, kb, HG * g + j, :],
                                     probs[:, kb % 2, j, 0:cols], start=(kb == 0), stop=(kb == NT - 1))
                last.then_inc(s["pv_done"], 1)

            def turn_heads(nb, batch, g, has):
                k = slot(("turn", g), nb, has)
                pe.wait_ge(s["o_copied"], at("o_copied", nb + batch, g + 1))
                for i in range(NT):
                    last = pe.transpose(pair[k][:, 0, i * P:(i + 1) * P], oT[:, i * P:(i + 1) * P], identf[:])
                last.then_inc(s["oT_ready"], 1)

            def turn_attn(nb, has):
                k = slot("attnT", nb, has)
                pe.wait_ge(s["attn_done"], at("attn_done", nb - 1, G))
                turn_tokens(attn, pair[k]).then_inc(s["attnT_ready"], 1)

            def project_back(nb, has):
                k = slot("proj", nb, has)
                pe.wait_ge(s["attnT_done"], at("attnT_done", nb - 1, 1))
                for i in range(NT):
                    for c in range(C):
                        last = pe.matmul(pair_flat[k][:, i * D:(i + 1) * D], attnT[:, c, i * P:(i + 1) * P],
                                         wo[:, c, :], start=(c == 0), stop=(c == C - 1))
                last.then_inc(s["proj_ready"], 1)

            def turn_normed(nb, has):
                k = slot("xn2T", nb, has)
                pe.wait_ge(s["r_norm"], at("r_norm", nb - 1, NT))
                turn_tokens(xn2, pair[k]).then_inc(s["xn2T_ready"], 1)

            def logits(m, nb):
                E = EXPERTS[m]
                pe.wait_ge(s["xn2T_done"], at("xn2T_done", nb - 1, 1))
                for i in range(NT):
                    for c in range(C):
                        last = pe.matmul(ps_logits[:, i * E:(i + 1) * E], xn2T[:, c, i * P:(i + 1) * P],
                                         gate[m][:, c, :], start=(c == 0), stop=(c == C - 1))
                last.then_inc(s["logits_ready"], 1)

            def prefix(m, b):
                E = EXPERTS[m]
                pe.wait_ge(route[m], (b - 1) * ROUTE[m] + MASKED[m])
                for i in range(NT):
                    dst = ps_prefix[:, i * E:(i + 1) * E]
                    pe.matmul(dst, tri[:, 0, :], mask_e[:, i, 0:E], start=True, stop=False)
                    for j in range(i):
                        pe.matmul(dst, tri[:, 1, :], mask_e[:, j, 0:E], start=False, stop=False)
                    last = pe.matmul(dst, tri[:, 1, :], before[m][:], start=False, stop=True)
                last.then_inc(s["prefix_ready"], 1)

            def step(m, b, par, has):
                nb = m * B + b
                for g2, batch2, g1 in ((3, LAST, 0), (0, NOW, 1), (1, NOW, 2), (2, NOW, 3)):
                    par2 = par if batch2 == NOW else 1 - par
                    if NOW in has:
                        first_pass(nb, g1, 0, has)
                        first_pass(nb, g1, 1, has)
                    for n in range(8):
                        if batch2 in has:
                            second_pass(nb, batch2, g2, n, has)
                        if n + 2 < 8 and NOW in has:
                            first_pass(nb, g1, n + 2, has)
                        if n == 1 and LAST in has:
                            if g1 == 1:
                                project_back(nb, has)
                            if g1 == 2:
                                logits(m, nb)
                        if n in (3, 5) and batch2 in has:
                            weigh_values(nb + batch2, par2, g2, n // 2 - 1)
                    if batch2 in has:
                        weigh_values(nb + batch2, par2, g2, 2)
                        weigh_values(nb + batch2, par2, g2, 3)
                    if NOW in has:
                        turn_max(nb, g1)
                    if batch2 in has:
                        turn_heads(nb, batch2, g2, has)
                    if g1 == 0:
                        if NEXT in has:
                            turn_next(nb, has)
                            project(nb, 0, has)
                        if LAST in has:
                            turn_attn(nb, has)
                        if NEXT in has:
                            project(nb, 1, has)
                    if g1 == 1:
                        if NEXT in has:
                            project(nb, 2, has)
                            project(nb, 3, has)
                        if LAST in has:
                            turn_normed(nb, has)
                    if g1 == 2:
                        if NEXT in has:
                            turn_chunk(m, nb, 0, has)
                            turn_chunk(m, nb, 1, has)
                        if LAST in has:
                            prefix(m, b)

            def plan(m):
                E, T = EXPERTS[m], BLOCKS[m]
                v, t = plan_v[m], plan_t[m]
                pe.wait_ge(route[m], B * ROUTE[m])
                pe.matmul(ps[0:E, 0, 0:1], before[m][:], tri[:, 1, 0:1], start=True, stop=True).then_inc(t, 1)
                pe.wait_ge(v, 2)
                pe.matmul(ps[0:E, 0, 8:9], tri_f[0:E, 1, 0:E], nblk[0:E, 1:2], start=True, stop=True).then_inc(t, 1)
                pe.wait_ge(v, 6)
                pe.matmul(ps[:, 1, 0:T], tri_f[0:E, 2, :], upto[0:E, 0:T], start=True, stop=True)
                pe.matmul(ps[:, 2, 0:T], nblk_row[0:E, :], upto[0:E, 0:T], start=True, stop=True)
                pe.matmul(ps[:, 3, 0:E], nblk_row[0:E, :], tri_f[0:E, 0, 0:E], start=True, stop=True)
                pe.matmul(ps[:, 4, 0:E], nblk_row[0:E, :], tri_f[0:E, 1, 0:E], start=True, stop=True)
                for h in range(-(-T // P)):
                    n = min(P, T - h * P)
                    last = pe.matmul(ps[0:n, 5, 2 * h:2 * h + 2], upto[0:E, h * P:h * P + n], onb[0:E, :],
                                     start=True, stop=True)
                last.then_inc(t, 1)
                pe.wait_ge(blk_in[m], 16 * -(-T // P))
                for h in range(-(-T // P)):
                    n = min(P, T - h * P)
                    last = pe.transpose(ps[:, 6, h * P:h * P + n], ids_f[0:n, h, :], identf[0:n, 0:n])
                last.then_inc(t, 1)

            def experts(m):
                E, T, K2 = EXPERTS[m], BLOCKS[m], HIDDEN[m]
                w = M[m]

                def turn_x(t, tq, r):
                    pe.wait_ge(w[f"gather{r}"], tq * 16 + 16)
                    if not (isinstance(t, int) and t < 2):
                        pe.wait_ge(w["xT_copied"], t - 1)
                    for c in range(C):
                        last = pe.transpose(ps[:, r % 2, c * P:(c + 1) * P], xg[:, r, c * P:(c + 1) * P], identf[:])
                    last.then_inc(w["x_turned"], 1)

                def expert_of(t):
                    if m == 0:
                        return pe.value_load(plan_i[0:1, 0, ds(t, 1)], min_val=0, max_val=E - 1)
                    return pe.value_load(plan_i[0:1, 1, ds(t, 1)], min_val=0, max_val=SLOTS - 1)

                def first_product(t, r):
                    e = expert_of(t)
                    if m == 1:
                        ready = pe.value_load(plan_i[0:1, 0, ds(t, 1)], min_val=0, max_val=E - 1)
                        pe.wait_ge(expert_in, ready * 32 + 32)
                        pe.sem_inc(own_wait, 1)
                    pe.wait_ge(w["xT_copied"], t + 1)
                    if not (isinstance(t, int) and t < 2):
                        pe.wait_ge(w["hid_done"], t - 1)
                    for c in range(C):
                        if m == 0:
                            rhs = w01[:, ds(e, 1), c, :].rearrange("p a n -> p (a n)")
                        else:
                            rhs = ring1[:, ds(e, 1), c * 192:(c + 1) * 192].rearrange("p a n -> p (a n)")
                        last = pe.matmul(ps[:, 2 + r % 2, 0:2 * K2], xgT[:, r % 2, c, :], rhs,
                                         start=(c == 0), stop=(c == C - 1))
                    last.then_inc(w["mm1_ready"], 1)

                def turn_h(t, r):
                    pe.wait_ge(w["hid_done"], t + 1)
                    if not (isinstance(t, int) and t < 2):
                        pe.wait_ge(w["hT_copied"], t - 1)
                    for c in range(-(-K2 // P)):
                        n = min(P, K2 - c * P)
                        last = pe.transpose(ps[0:n, 4 + r % 2, c * P:(c + 1) * P], hid[:, r % 2, c * P:c * P + n],
                                            identf[:])
                    last.then_inc(w["h_turned"], 1)

                def second_product(t, r):
                    e = expert_of(t)
                    pe.wait_ge(w["hT_copied"], t + 1)
                    if not (isinstance(t, int) and t < 2):
                        pe.wait_ge(w["y_copied"], t - 1)
                    if m == 0:
                        for c in range(2):
                            last = pe.matmul(ps[:, 6 + r % 2, 0:D], hidT[:, r % 2, c, :],
                                             wout[:, ds(e, 1), c, :].rearrange("p a n -> p (a n)"),
                                             start=(c == 0), stop=(c == 1))
                    else:
                        last = pe.matmul(ps[:, 6 + r % 2, 0:D], hidT[0:K2, r % 2, 0, :],
                                         ring1[0:K2, ds(e, 1), 384:640].rearrange("p a n -> p (a n)"),
                                         start=True, stop=True)
                    last.then_inc(w["mm2_ready"], 1)

                def body(t, r, tq1, turn=True):
                    turn_h(t - 1, (r - 1) % 4)
                    if turn:
                        turn_x(t + 1, tq1, (r + 1) % 4)
                    first_product(t, r)
                    second_product(t - 1, (r - 1) % 4)

                pe.wait_ge(plan_v[m], PLAN_IDS)
                if m == 0:
                    pe.wait_ge(w0_in, 32)
                turn_x(0, 0, 0)
                turn_x(1, 0, 1)
                first_product(0, 0)
                for t in range(1, 5):
                    body(t, t % 4, (t + 1) // 4)
                with pe.Fori(1, (T - 4) // 4) as q:
                    for r in range(4):
                        body(q * 4 + (r + 1), (r + 1) % 4, q + (1 if r >= 2 else 0))
                for t in range(T - 3, T):
                    body(t, t % 4, (t + 1) // 4, turn=t + 1 < T)
                turn_h(T - 1, (T - 1) % 4)
                second_product(T - 1, (T - 1) % 4)

            pe.wait_ge(const_in, 16 * 9)
            pe.wait_ge(iotas, 14)
            for m in range(2):
                pe.wait_ge(w_in[m], 32)
                step(m, -1, 1, (NEXT,))
                step(m, 0, 0, (NOW, NEXT))
                with pe.Fori(0, B // 2 - 1) as q:
                    step(m, q * 2 + 1, 1, (LAST, NOW, NEXT))
                    step(m, q * 2 + 2, 0, (LAST, NOW, NEXT))
                step(m, B - 1, 1, (LAST, NOW))
                step(m, B, 0, (LAST,))
                plan(m)
                experts(m)

        @block.scalar
        def _(act_):
            def copy_xnT(nb):
                act_.wait_ge(s["xnT_ready"], at("xnT_ready", nb, 1))
                act_.copy(xnT[:].rearrange("p c t -> p (c t)"), pair_flat[UNIT["xnT"] % 3]).then_inc(s["xnT_done"], 1)

            def copy_qkv(m, nb, par, i):
                k = UNIT[("qkv", i)] % 3
                act_.wait_ge(s["qkv_ready"], at("qkv_ready", nb, i + 1))
                if m == 0:
                    if i >= 2:
                        act_.wait_ge(s["rope_done"], at("rope_done", nb, i - 1))
                    act_.copy(qk_raw[:, i % 2, :], pair[k][:, 0, :]).then_inc(s["qk_copied"], 1)
                else:
                    act_.copy(qk[:, i, :], pair[k][:, 0, :]).then_inc(s["qk_copied"], 1)
                act_.copy(values[:, par, i, :, 0:DH], pair[k][:, 1, 0:D].rearrange("p (h d) -> p h d", h=H))\
                    .then_inc(s["v_copied"], 1)

            def first_part(nb, cp):
                act_.wait_ge(s["chunk_ready"], at("chunk_ready", nb, cp + 1))
                for stored in ("qk_stored", "k_stored"):
                    after_first(act_, s[stored], at(stored, nb, 0))
                act_.copy(parts[:, 0, 2 * cp:2 * cp + 2, :], pair[UNIT[("chunk", cp)] % 3]).then_inc(s["part1"], 1)

            def second_part(nb, cp):
                act_.wait_ge(s["rest1"], at("rest1", nb, cp + 1))
                act_.copy(parts[:, 1, 2 * cp:2 * cp + 2, :].rearrange("p c t -> p (c t)"), rest[:, cp, :])\
                    .then_inc(s["part2"], 1)

            def turned_max(nb, g):
                act_.wait_ge(s["mT_ready"], at("mT_ready", nb, g + 1))
                after_first(act_, max_in[(g - 2) % G], nb * 16 + (16 if g >= 2 else 0))
                act_.copy(maxT[:, g % 2, :], ps_max).then_inc(s["mT_done"], 1)
                act_.wait_ge(s["mT_done"], at("mT_done", nb, g + 1))
                act_.dma_start(q_stack[ROWS:ROWS + 3, HG * g:HG * g + HG, :].rearrange(
                    "j h (a t) -> j (h a) t", t=P), maxT[:, g % 2, :]).then_inc(max_in[g], 16)

            def exponentials(nb, g, n):
                kb, p = divmod(n, 2)
                act_.wait_ge(s["s2_ready"], at("s2_ready", nb, 8 * g + n + 1))
                after_first(act_, s["pv_done"], at("pv_done", nb, 4 * g + kb - 1))
                cols = S - kb * P
                act_.activation(probs[:, kb % 2, 2 * p:2 * p + 2, 0:cols], pair[UNIT[("p2", g, n)] % 3][:, :, 0:cols],
                                ACT.Exp, scale=SCALE).then_inc(s["exp_done"], 1)

            def copy_heads(nb, g):
                act_.wait_ge(s["pv_done"], at("pv_done", nb, 4 * g + 4))
                after_first(act_, s["oT_ready"], at("oT_ready", nb, g))
                act_.copy(oT[:], ps_o).then_inc(s["o_copied"], 1)

            def copy_turned(name, dst, nb):
                act_.wait_ge(s[f"{name}_ready"], at(f"{name}_ready", nb, 1))
                act_.copy(dst[:].rearrange("p c t -> p (c t)"), pair_flat[UNIT[name] % 3])\
                    .then_inc(s[f"{name}_done"], 1)

            def router(m, b):
                if m == 0:
                    act_.wait_ge(route[0], b * ROUTE[0] + 2 * NT + 2)
                    act_.activation(r_exp[:, :, 0:2], r_prob[:, :, 0:2], ACT.Exp).then_inc(r_exp_done[0], 1)
                else:
                    act_.wait_ge(route[1], b * ROUTE[1] + 1)
                    for i in range(NT):
                        act_.activation(r_exp[:, i, :], ps_logits[:, i * 64:(i + 1) * 64], ACT.Exp,
                                        bias=r_max[:, i:i + 1], accum_out=r_sum[:, i:i + 1]).then_inc(r_exp_done[1], 1)

            def step(m, b, par, has):
                nb = m * B + b
                for g2, batch2, g1 in ((3, LAST, 0), (0, NOW, 1), (1, NOW, 2), (2, NOW, 3)):
                    for n in range(8):
                        if batch2 in has:
                            exponentials(nb + batch2, g2, n)
                        if g1 == 2 and n == 3 and LAST in has:
                            router(m, b - 1)
                    if NOW in has:
                        turned_max(nb, g1)
                    if batch2 in has:
                        copy_heads(nb + batch2, g2)
                    if g1 == 0:
                        if NEXT in has:
                            copy_xnT(nb + 1)
                            copy_qkv(m, nb + 1, 1 - par, 0)
                        if LAST in has:
                            copy_turned("attnT", attnT, nb - 1)
                        if NEXT in has:
                            copy_qkv(m, nb + 1, 1 - par, 1)
                    if g1 == 1:
                        if NEXT in has:
                            copy_qkv(m, nb + 1, 1 - par, 2)
                            copy_qkv(m, nb + 1, 1 - par, 3)
                        if LAST in has:
                            copy_turned("xn2T", xn2T, nb - 1)
                    if g1 == 2 and NEXT in has:
                        first_part(nb + 1, 0)
                        first_part(nb + 1, 1)
                        second_part(nb + 1, 0)
                        second_part(nb + 1, 1)

            def experts(m):
                T, K2 = BLOCKS[m], HIDDEN[m]
                w = M[m]

                def silu(t, r):
                    act_.wait_ge(w["mm1_ready"], t + 1)
                    act_.activation(act[:, r % 2, 0:K2], ps[:, 2 + r % 2, 0:K2], ACT.Silu).then_inc(w["silu_done"], 1)

                def copy_h(t, r):
                    act_.wait_ge(w["h_turned"], t + 1)
                    n = min(P, K2)
                    act_.copy(hidT[0:n, r % 2, 0:-(-K2 // P), :],
                              ps[0:n, 4 + r % 2, 0:-(-K2 // P) * P].rearrange("p (c t) -> p c t", t=P))\
                        .then_inc(w["hT_copied"], 1)

                def copy_y(t, r, th):
                    act_.wait_ge(w["mm2_ready"], t + 1)
                    if not (isinstance(t, int) and t < 2):
                        act_.wait_ge(w[f"y_store{r % 2}"], th * 16)
                    act_.copy(y[:, r % 2, :], ps[:, 6 + r % 2, 0:D]).then_inc(w["y_copied"], 1)
                    act_.wait_ge(w["y_copied"], t + 1)
                    act_.dma_start(y_dram[m][ds(t * P, P), :], y[:, r % 2, :]).then_inc(w[f"y_store{r % 2}"], 16)

                silu(0, 0)
                for r in range(4):
                    copy_h(r, r)
                    silu(r + 1, (r + 1) % 4)
                    copy_y(r, r, r // 2)
                with act_.Fori(1, (T - 4) // 4) as q:
                    for r in range(4):
                        copy_h(q * 4 + r, r)
                        silu(q * 4 + (r + 1), (r + 1) % 4)
                        copy_y(q * 4 + r, r, q * 2 + r // 2)
                for t in range(T - 3, T):
                    copy_h(t - 1, (t - 1) % 4)
                    silu(t, t % 4)
                    copy_y(t - 1, (t - 1) % 4, (t - 1) // 2)
                copy_h(T - 1, (T - 1) % 4)
                copy_y(T - 1, (T - 1) % 4, (T - 1) // 2)

            for m in range(2):
                act_.wait_ge(ids_zero[m], 16)
                step(m, -1, 1, (NEXT,))
                step(m, 0, 0, (NOW, NEXT))
                with act_.Fori(0, B // 2 - 1) as q:
                    step(m, q * 2 + 1, 1, (LAST, NOW, NEXT))
                    step(m, q * 2 + 2, 0, (LAST, NOW, NEXT))
                step(m, B - 1, 1, (LAST, NOW))
                step(m, B, 0, (LAST,))
                experts(m)

        @block.vector
        def _(v):
            def moments(k, nb, b):
                for i in range(NT):
                    v.bn_stats(stats[k][:, i, :], x[:, ds(NT * b + i, 1), :].rearrange("p a d -> p (a d)"))\
                        .then_inc(s[f"{k}_stats"], 1)
                v.wait_ge(s[f"{k}_stats"], at(f"{k}_stats", nb, NT))
                v.sem_inc(own_wait, 1)
                for i in range(NT):
                    v.bn_aggr(mean_var[k][:, i, :], stats[k][:, i, :]).then_inc(s[f"{k}_aggr"], 1)

            def normalise(k, dst, nb, b):
                v.wait_ge(s[f"{k}_rstd"], at(f"{k}_rstd", nb, 1))
                for i in range(NT):
                    v.tensor_scalar(dst[:, i, :], x[:, ds(NT * b + i, 1), :].rearrange("p a d -> p (a d)"),
                                    mean_var[k][:, i, 0:1], rstd[k][:, i:i + 1], ALU.subtract, ALU.mult)\
                        .then_inc(s[f"{k}_norm"], 1)

            def maximum(nb, g, n):
                qb, p = divmod(n, 2)
                k = UNIT[("p1", g, n)] % 3
                v.wait_ge(s["s1_ready"], at("s1_ready", nb, 8 * g + n + 1))
                v.tensor_reduce(neg_max[:, g % 2, 2 * p:2 * p + 2, qb:qb + 1], pair[k][:, :, 0:(qb + 1) * P], AX,
                                ALU.max, negate=True).then_inc(s["max_done"], 1)

            def split_max(nb, g):
                src = neg_max[:, g % 2, :, :].rearrange("p h q -> p (h q)")
                parts_, r = max_parts[:, g % 2], max_rest[:, g % 2, :]
                v.wait_ge(s["max_done"], at("max_done", nb, 8 * g + 8))
                v.tensor_copy(parts_[:, 0, :], src).then_inc(s["m_split"], 1)
                v.wait_ge(s["m_split"], at("m_split", nb, 4 * g + 1))
                v.tensor_tensor(r, src, parts_[:, 0, :], ALU.subtract).then_inc(s["m_split"], 1)
                v.wait_ge(s["m_split"], at("m_split", nb, 4 * g + 2))
                v.tensor_copy(parts_[:, 1, :], r).then_inc(s["m_split"], 1)
                v.wait_ge(s["m_split"], at("m_split", nb, 4 * g + 3))
                v.tensor_tensor(parts_[:, 2, :], r, parts_[:, 1, :], ALU.subtract).then_inc(s["m_split"], 1)

            def rotated(nb, i):
                v.wait_ge(s["rope_cos"], at("rope_cos", nb, i + 1))
                v.wait_ge(s["rope_swap"], at("rope_swap", nb, 2 * i + 2))
                v.tensor_tensor(qk[:, i, :], rope[:, 0, :], rope[:, 1, :], ALU.add).then_inc(s["rope_done"], 1)

            def less_first_part(nb, cp):
                v.wait_ge(s["part1"], at("part1", nb, cp + 1))
                v.tensor_tensor(rest[:, cp, :], pair_flat[UNIT[("chunk", cp)] % 3],
                                parts[:, 0, 2 * cp:2 * cp + 2, :].rearrange("p c t -> p (c t)"), ALU.subtract)\
                    .then_inc(s["rest1"], 1)

            def divide(nb, g):
                heads = pair[UNIT[("turn", g)] % 3][:, 0, :].rearrange("p (i h d) -> p i h d", i=NT, h=HG)
                v.wait_ge(s["oT_ready"], at("oT_ready", nb, g + 1))
                v.reciprocal(rec[:].rearrange("p i (h a) -> p i h a", a=1), heads[:, :, :, DH:DH + 1])\
                    .then_inc(s["rec_done"], 1)
                v.wait_ge(s["rec_done"], at("rec_done", nb, g + 1))
                if g == 0:
                    after_first(v, s["attnT_ready"], at("attnT_ready", nb, 0))
                v.tensor_tensor(attn[:, :, 64 * g:64 * g + 64].rearrange("p i (h d) -> p i h d", h=HG),
                                heads[:, :, :, 0:DH],
                                rec[:].rearrange("p i (h a) -> p i h a", a=1).to_broadcast([P, NT, HG, DH]),
                                ALU.mult).then_inc(s["attn_done"], 1)

            def add_residual(nb, b):
                rows = x[:, ds(NT * b, NT), :].rearrange("p i d -> p (i d)")
                v.wait_ge(s["proj_ready"], at("proj_ready", nb, 1))
                v.tensor_tensor(rows, pair_flat[UNIT["proj"] % 3], rows, ALU.add).then_inc(s["resid_done"], 1)

            def step(m, b, has):
                nb = m * B + b
                for g1, g2, batch2 in ((0, 3, LAST), (1, 0, NOW), (2, 1, NOW), (3, 2, NOW)):
                    for n in range(8):
                        if NOW in has:
                            maximum(nb, g1, n)
                        if NEXT in has:
                            if g1 == 0 and n == 2:
                                v.sem_inc(own_wait, 1)
                                moments("a", nb + 1, b + 1)
                            if g1 == 0 and n == 4:
                                after_first(v, s["xn_stored"], at("xn_stored", nb - 1, 0))
                                normalise("a", xn, nb + 1, b + 1)
                            if m == 0 and g1 in (1, 2) and n in (1, 4):
                                rotated(nb + 1, 2 * (g1 - 1) + n // 4)
                        if LAST in has:
                            if g1 == 1 and n == 3:
                                add_residual(nb - 1, b - 1)
                                v.wait_ge(s["resid_done"], at("resid_done", nb - 1, 1))
                                v.sem_inc(own_wait, 1)
                                moments("r", nb - 1, b - 1)
                            if g1 == 1 and n == 6:
                                if NEXT in has:
                                    v.wait_ge(s["xnT_ready"], at("xnT_ready", nb + 1, 1))
                                else:
                                    v.wait_ge(s["xn_stored"], at("xn_stored", nb - 1, 0))
                                normalise("r", xn2, nb - 1, b - 1)
                            if g1 == 2 and n == 3:
                                rank(m, b - 1)
                            if g1 == 2 and n == 6:
                                weigh(m, b - 1)
                            if g1 == 3 and n == 2:
                                place(m, b - 1)
                    if NOW in has:
                        split_max(nb, g1)
                    if g1 == 2 and LAST in has:
                        mark(m, b - 1)
                    if batch2 in has:
                        divide(nb + batch2, g2)
                    if g1 == 2 and NEXT in has:
                        less_first_part(nb + 1, 0)
                        less_first_part(nb + 1, 1)

            col = lambda a: a.rearrange("p (i a) -> p i a", a=1)

            def held():
                v.sem_inc(own_wait, 1)

            def counted(m, b, start):
                done = [start]

                def step_(ins, wait=True):
                    done[0] += 1
                    ins.then_inc(route[m], 1)
                    if wait:
                        v.wait_ge(route[m], b * ROUTE[m] + done[0])
                return step_, done

            def best(m, b, step_, done, ranked):
                for i in range(NT):
                    step_(v.max(top[:, i, :], ranked[i]), wait=False)
                v.wait_ge(route[m], b * ROUTE[m] + done[0])
                held()
                for i in range(NT):
                    step_(v.max_index(top_i[:, i, :], top[:, i, :], ranked[i]), wait=False)

            def rank(m, b):
                E, K, nb = EXPERTS[m], CHOICES[m], m * B + b
                step_, done = counted(m, b, 0)
                logits = ps_logits[:, 0:NT * E].rearrange("p (i e) -> p i e", i=NT)
                v.wait_ge(s["logits_ready"], at("logits_ready", nb, 1))
                if m == 0:
                    held()
                    best(m, b, step_, done, [logits[:, i, :] for i in range(NT)])
                    step_(v.tensor_scalar(r_max[:], top[:, :, 0], -1.0, None, ALU.mult))
                    step_(v.tensor_tensor(r_prob[:, :, 0:K], top[:, :, 0:K], col(r_max[:]).to_broadcast([P, NT, K]),
                                          ALU.add), wait=False)
                else:
                    step_(v.tensor_reduce(col(r_max[:]), logits, AX, ALU.max, negate=True), wait=False)
                assert done[0] == RANKED[m]

            def weigh(m, b):
                E, K = EXPERTS[m], CHOICES[m]
                step_, done = counted(m, b, RANKED[m])
                if m == 0:
                    v.wait_ge(r_exp_done[0], b + 1)
                    num = r_exp[:, :, 0:K]
                    step_(v.tensor_reduce(col(r_sum[:]), num, AX, ALU.add))
                else:
                    v.wait_ge(r_exp_done[1], b * NT + NT)
                    step_(v.reciprocal(r_inv[:], r_sum[:]))
                    step_(v.tensor_tensor(r_prob[:], r_exp[:], col(r_inv[:]).to_broadcast([P, NT, E]), ALU.mult))
                    held()
                    best(m, b, step_, done, [r_prob[:, i, :] for i in range(NT)])
                    num = top[:, :, 0:K]
                    step_(v.tensor_reduce(col(r_sum[:]), num, AX, ALU.add))
                    step_(v.tensor_scalar(r_sum[:], r_sum[:], 1e-12, None, ALU.max))
                step_(v.reciprocal(r_inv[:], r_sum[:]))
                step_(v.tensor_tensor(weight_all[:, ds(NT * b, NT), 0:K], num,
                                      col(r_inv[:]).to_broadcast([P, NT, K]), ALU.mult), wait=False)
                assert done[0] == WEIGHED[m]

            def mark(m, b):
                E, K = EXPERTS[m], CHOICES[m]
                step_, done = counted(m, b, WEIGHED[m])
                step_(v.tensor_copy(chosen[:, :, 0:K], top_i[:, :, 0:K]))
                with nc.allow_low_precision(reason="zeros and ones"):
                    step_(v.tensor_tensor(
                        onehot[:, :, 0:K, 0:E],
                        iota_e[:, 0:E].rearrange("p (a b e) -> p a b e", a=1, b=1).to_broadcast([P, NT, K, E]),
                        chosen[:, :, 0:K].rearrange("p i (k a) -> p i k a", a=1).to_broadcast([P, NT, K, E]),
                        ALU.is_equal))
                    step_(v.tensor_reduce(mask_e[:, :, 0:E].rearrange("p i (e a) -> p i e a", a=1),
                                          onehot[:, :, 0:K, 0:E].rearrange("p i k e -> p i e k"), AX, ALU.add),
                          wait=False)
                assert done[0] == MASKED[m]

            def place(m, b):
                E, K, nb = EXPERTS[m], CHOICES[m], m * B + b
                step_, done = counted(m, b, MASKED[m])
                hot = onehot[:, :, 0:K, 0:E]
                v.wait_ge(s["prefix_ready"], at("prefix_ready", nb, 1))
                where = place_e[:, :, 0:E]
                step_(v.tensor_tensor(where, ps_prefix[:, 0:NT * E].rearrange("p (i e) -> p i e", i=NT),
                                      base_e[:, 0:E].rearrange("p (a e) -> p a e", a=1).to_broadcast([P, NT, E]),
                                      ALU.add))
                pick = picked[:, 0:NT * K * E].rearrange("p (i k e) -> p i k e", i=NT, k=K)
                step_(v.tensor_tensor(pick, hot, where.rearrange("p i (a e) -> p i a e", a=1)
                                      .to_broadcast([P, NT, K, E]), ALU.mult))
                step_(v.tensor_reduce(dest_f[:, :, 0:K].rearrange("p i (k a) -> p i k a", a=1), pick, AX, ALU.add))
                step_(v.tensor_copy(dest_all[:, ds(NT * b, NT), 0:K], dest_f[:, :, 0:K]), wait=False)
                step_(v.tensor_copy(expert_all[:, ds(NT * b, NT), 0:K], chosen[:, :, 0:K]), wait=False)
                step_(v.tensor_reduce(tile_sum[:, 0:E].rearrange("p (e a) -> p e a", a=1),
                                      mask_e[:, :, 0:E].rearrange("p i e -> p e i"), AX, ALU.add))
                step_(v.tensor_tensor(before[m][:], before[m][:], tile_sum[:, 0:E], ALU.add))
                after_first(v, scattered[m], b * (16 * NT * K))
                held()
                step_(v.tensor_copy(dest[:, :, 0:K], dest_f[:, :, 0:K]), wait=False)
                assert done[0] == ROUTE[m], (done, ROUTE)

            def plan(m):
                E, K, T = EXPERTS[m], CHOICES[m], BLOCKS[m]
                sv, st = plan_v[m], plan_t[m]
                done = [0]

                def step(ins, wait=True):
                    done[0] += 1
                    ins.then_inc(sv, 1)
                    if wait:
                        v.wait_ge(sv, done[0])

                v.wait_ge(st, 1)
                step(v.tensor_scalar(more[0:E, :], iota_j[0:E, :], ps[0:E, 0, 0:1], None, ALU.is_lt))
                v.wait_ge(sv, 1)
                v.tensor_reduce(nblk[0:E, 0:1], more[0:E, :], AX, ALU.add).then_inc(iotas, 1)
                v.wait_ge(iotas, 15 + m)
                step(v.tensor_scalar(nblk[0:E, 1:2], nblk[0:E, 0:1], 1.0, None, ALU.max))
                v.wait_ge(st, 2)
                step(v.tensor_scalar(upto[0:E, 0:T], iota_t[0:E, 0:T], ps[0:E, 0, 8:9], None, ALU.is_ge))
                step(v.tensor_scalar(nblk_row[0:E, :], tri_f[0:E, 2, :], nblk[0:E, 1:2], None, ALU.mult))
                step(v.tensor_copy(onb[0:E, 0:1], tri_f[0:E, 2, 0:1]))
                step(v.tensor_copy(onb[0:E, 1:2], nblk[0:E, 1:2]))
                v.wait_ge(st, 3)
                n = -(-T // P)
                for h in range(n):
                    r = min(P, T - h * P)
                    step(v.tensor_scalar(blk_f[0:r, h, :], ps[0:r, 5, 2 * h:2 * h + 2], 1.0, None, ALU.mult))
                    step(v.tensor_scalar(blk_f[0:r, h, 1:2], iota_p[0:r, h:h + 1], blk_f[0:r, h, 1:2], 31.0,
                                         ALU.subtract, ALU.min))
                    step(v.tensor_scalar(blk_f[0:r, h, 0:1], blk_f[0:r, h, 0:1], float(E - 1), float(TOK // P),
                                         ALU.min, ALU.mult))
                    step(v.tensor_tensor(blk_f[0:r, h, 0:1], blk_f[0:r, h, 0:1], blk_f[0:r, h, 1:2], ALU.add))
                    step(v.tensor_copy(blk_i[0:r, h:h + 1], blk_f[0:r, h, 0:1]))
                for _ in range(2 - n):
                    for _ in range(5):
                        step(v.tensor_copy(corr[:, 0:1], iota_e[:, 0:1]))
                assert done[0] == PLAN_BLOCKS
                step(v.tensor_scalar(plan_f[:, 0:T], ps[:, 1, 0:T], float(E - 1), None, ALU.min))
                step(v.tensor_copy(plan_i[:, 0, 0:T], plan_f[:, 0:T]))
                step(v.tensor_scalar(plan_i[:, 1, 0:T], plan_i[:, 0, 0:T], SLOTS - 1, None, ALU.bitwise_and))
                step(v.tensor_copy(plan_i[:, 2, 0:E], ps[:, 4, 0:E]))
                assert done[0] == PLAN_READY
                step(v.tensor_scalar(corr[:, 0:E], ps[:, 3, 0:E], float(P), None, ALU.mult))
                step(v.tensor_tensor(corr[:, 0:E], corr[:, 0:E], base_e[:, 0:E], ALU.subtract))
                v.wait_ge(st, 4)
                step(v.tensor_copy(ids[:, 0:T], ps[:, 6, 0:T]))
                assert done[0] == PLAN_IDS
                per = min(TILES // 2, 1024 // (K * E))
                n0 = done[0]
                with v.Fori(0, TILES // per) as q:
                    hot = onehot[:].rearrange("p i k e -> p (i k e)")[:, 0:per * K * E].rearrange(
                        "p (i k e) -> p i k e", i=per, k=K)
                    pick = picked[:, 0:per * K * E].rearrange("p (i k e) -> p i k e", i=per, k=K)
                    who = expert_all[:, ds(q * per, per), 0:K]
                    v.wait_ge(sv, q * 4 + n0)
                    v.tensor_tensor(
                        hot, iota_e[:, 0:E].rearrange("p (a b e) -> p a b e", a=1, b=1).to_broadcast([P, per, K, E]),
                        who.rearrange("p i (k a) -> p i k a", a=1).to_broadcast([P, per, K, E]),
                        ALU.is_equal).then_inc(sv, 1)
                    v.wait_ge(sv, q * 4 + (n0 + 1))
                    v.tensor_tensor(pick, hot, corr[:, 0:E].rearrange("p (a b e) -> p a b e", a=1, b=1)
                                    .to_broadcast([P, per, K, E]), ALU.mult).then_inc(sv, 1)
                    v.wait_ge(sv, q * 4 + (n0 + 2))
                    v.sem_inc(own_wait, 1)
                    v.tensor_reduce(expert_all[:, ds(q * per, per), 0:K].rearrange("p i (k a) -> p i k a", a=1),
                                    pick, AX, ALU.add).then_inc(sv, 1)
                    v.wait_ge(sv, q * 4 + (n0 + 3))
                    v.tensor_tensor(slot_all[:, ds(q * per, per), 0:K], expert_all[:, ds(q * per, per), 0:K],
                                    dest_all[:, ds(q * per, per), 0:K], ALU.add).then_inc(sv, 1)

            def experts(m):
                T, K2 = BLOCKS[m], HIDDEN[m]
                w = M[m]

                def copy_x(t, r):
                    v.wait_ge(w["x_turned"], t + 1)
                    v.tensor_copy(xgT[:, r % 2, :, :].rearrange("p c t -> p (c t)"), ps[:, r % 2, 0:D])\
                        .then_inc(w["xT_copied"], 1)

                def gated(t, r):
                    v.wait_ge(w["silu_done"], t + 1)
                    v.tensor_tensor(hid[:, r % 2, 0:K2], ps[:, 2 + r % 2, K2:2 * K2], act[:, r % 2, 0:K2], ALU.mult)\
                        .then_inc(w["hid_done"], 1)

                copy_x(0, 0)
                copy_x(1, 1)
                gated(0, 0)
                with v.Fori(0, (T - 4) // 4) as q:
                    for r in range(4):
                        copy_x(q * 4 + (r + 2), (r + 2) % 4)
                        gated(q * 4 + (r + 1), (r + 1) % 4)
                for t in range(T - 3, T):
                    if t + 1 < T:
                        copy_x(t + 1, (t + 1) % 4)
                    gated(t, t % 4)

            def add_back(m):
                K = CHOICES[m]
                per = RING // K
                used = M[m]["back_used"]
                rounds0 = 0 if m == 0 else TILES * CHOICES[0] // RING
                with v.Fori(0, TILES // per) as q:
                    for r in range(RING):
                        i, k = divmod(r, K)
                        row = x[:, ds(q * per + i, 1), :].rearrange("p a d -> p (a d)")
                        v.wait_ge(back_in[r], (q + rounds0) * 16 + 16)
                        if k:
                            v.wait_ge(used, q * RING + r)
                        v.scalar_tensor_tensor(
                            out=row, in0=back[:, r, :], scalar=weight_all[:, ds(q * per + i, 1), k:k + 1]
                            .rearrange("p a k -> p (a k)"), in1=row, op0=ALU.mult, op1=ALU.add).then_inc(used, 1)

            v.memset(tri_f[:, 2, :], 1.0).then_inc(iotas, 1)
            v.wait_ge(const_in, 16 * 9)
            v.tensor_copy(tri_f[:, 0, :], tri[:, 0, :]).then_inc(iotas, 1)
            v.wait_ge(iotas, 9)
            v.tensor_tensor(tri_f[:, 1, :], tri_f[:, 0, :], identf[:], ALU.add).then_inc(iotas, 1)
            v.memset(k_stack[ROWS:ROWS + 3, :, :], 1.0).then_inc(iotas, 1)
            v.memset(before[0][:], 0.0).then_inc(iotas, 1)
            v.memset(before[1][:], 0.0).then_inc(iotas, 1)
            v.memset(values[:, :, :, :, DH:DH + 1], 1.0).then_inc(iotas, 1)
            v.wait_ge(iotas, 14)
            v.wait_ge(x_in0, 16)
            v.wait_ge(x_in1, 16)
            for m in range(2):
                step(m, -1, (NEXT,))
                step(m, 0, (NOW, NEXT))
                with v.Fori(1, B - 1) as b:
                    step(m, b, (LAST, NOW, NEXT))
                step(m, B - 1, (LAST, NOW))
                step(m, B, (LAST,))
                plan(m)
                experts(m)
                add_back(m)


RANKED = (10, 1)
WEIGHED = (13, 15)
MASKED = (16, 18)
PLAN_BLOCKS = 16
PLAN_READY = 20
PLAN_IDS = 23


def kernel(**inputs):
    import math
    import ml_dtypes
    import numpy as np
    from concourse import bacc, mybir as mb
    from concourse.bass_utils import run_bass_kernel_spmd

    a = {k: np.asarray(v) for k, v in inputs.items()}
    chunks = lambda w: np.ascontiguousarray(w.reshape(C, P, w.shape[-1]).transpose(1, 0, 2))
    each = lambda w: np.ascontiguousarray(w.reshape(w.shape[0], C, P, w.shape[-1]).transpose(0, 2, 1, 3))
    arrays = {
        "x": a["L0_attn_x"].reshape(TILES, P, D).transpose(1, 0, 2),
        "wqkv0": chunks(a["L0_attn_Wqkv"].T), "wqkv1": chunks(a["L1_attn_Wqkv"]),
        "wo0": chunks(a["L0_attn_WO"].T), "wo1": chunks(a["L1_attn_Wo"]),
        "gate0": chunks(a["L0_ffn_gate_kernel"]), "gate1": chunks(a["L1_ffn_gate_weight"].T),
        "w01_0": each(np.concatenate([a["L0_ffn_wi_0"], a["L0_ffn_wi_1"]], axis=2)).transpose(1, 0, 2, 3),
        "wout_0": each(a["L0_ffn_wo"]).transpose(1, 0, 2, 3),
        "w01_1": each(a["L1_ffn_gate_up_proj"].transpose(0, 2, 1)).reshape(EXPERTS[1], P, C * 2 * HIDDEN[1]),
        "wout_1": a["L1_ffn_down_proj"].transpose(0, 2, 1),
    }
    pos = np.arange(S, dtype=np.float32)
    freqs = np.exp(np.float32(-math.log(10000.0)) * np.arange(0, DH, 2, dtype=np.float32) / np.float32(DH))
    angles = (pos[:, None] * freqs[None, :].astype(np.float32)).astype(np.float32)
    sign = np.tile(np.array([-1.0, 1.0], np.float32), DH // 2)
    by_tile = lambda t: t.reshape(NT, P, DH).transpose(1, 0, 2)
    arrays["cos"] = by_tile(np.repeat(np.cos(angles), 2, axis=1).astype(np.float32))
    arrays["sin"] = by_tile((np.repeat(np.sin(angles), 2, axis=1) * sign).astype(np.float32))
    row, col = np.arange(P)[:, None], np.arange(P)[None, :]
    arrays["identf"] = np.eye(P, dtype=np.float32)
    arrays["identb"] = np.eye(P, dtype=np.float32).astype(ml_dtypes.bfloat16)
    arrays["masks"] = np.stack([np.where(col > row, -1e30, 0.0), np.where(row > col, -1e30, 0.0)], axis=1)\
        .astype(ml_dtypes.bfloat16)
    arrays["tri"] = np.stack([(row < col).astype(np.float32), np.ones((P, P), np.float32)], axis=1)\
        .astype(ml_dtypes.bfloat16)
    arrays["token"] = (np.arange(TILES)[None, :] * P + row).astype(np.float32)
    arrays = {f"in_{k}": np.ascontiguousarray(v) for k, v in arrays.items()}

    nc = bacc.Bacc("TRN2", target_bir_lowering=False, num_devices=1)
    t = {k[3:]: nc.dram_tensor(k, v.shape, mb.dt.from_np(v.dtype), kind="ExternalInput").ap()
         for k, v in arrays.items()}
    out = nc.dram_tensor("out", (P, TILES, D), mb.dt.float32, kind="ExternalOutput").ap()
    two = lambda k: [t[f"{k}0"], t[f"{k}1"]]
    two_moe_layers(nc, t["x"], two("wqkv"), two("wo"), two("gate"), two("w01_"), two("wout_"), t["cos"], t["sin"],
                   t["identf"], t["identb"], t["masks"], t["tri"], t["token"], out)
    r = run_bass_kernel_spmd(nc, [arrays], core_ids=[0])
    return np.ascontiguousarray(r.results[0]["out"].transpose(1, 0, 2)).reshape(B, S, D)
```
